# Optimizing a Trainium2 kernel written in Bass

```python
import numpy as np
import jax
import jax.numpy as jnp

def _softmax(x, axis=-1):
    return jax.nn.softmax(x, axis=axis)

def _gelu(x):
    return jax.nn.gelu(x, approximate=True)

def _silu(x):
    return jax.nn.silu(x)

def _sigmoid(x):
    return jax.nn.sigmoid(x)

def _layernorm(x, axis=-1, eps=1e-05):
    m = jnp.mean(x, axis=axis, keepdims=True)
    v = jnp.var(x, axis=axis, keepdims=True)
    return (x - m) / jnp.sqrt(v + eps)

def _scatter_add(tgt, idx, src, axis=0):
    return tgt.at[idx].add(src)

def _segment_sum(src, seg, n):
    return jax.ops.segment_sum(src, seg, n)
kernel_name = 'mk_gnn_preln_d4_gnn_r32_c96c5f'

def setup_inputs(seed: int=0):
    np.random.seed(seed)
    _w = jnp.asarray

    def _rec_inputs():
        import jax
        import jax.numpy as jnp
        _gk = jax.random.key(seed)
        x = -0.000202 + 1 * jax.random.normal(jax.random.fold_in(_gk, 1), (3125, 64), jnp.float32)
        src = jax.random.randint(jax.random.fold_in(_gk, 2), (100000,), 0, 3125, jnp.int32)
        dst = jax.random.randint(jax.random.fold_in(_gk, 3), (100000,), 0, 3125, jnp.int32)
        _o = jnp.argsort(dst, stable=True)
        src = src[_o]
        dst = dst[_o]
        edge_type_200 = jax.random.randint(jax.random.fold_in(_gk, 13), (100000,), 0, 200, jnp.int32)
        edge_weight = jax.random.uniform(jax.random.fold_in(_gk, 14), (100000,), jnp.float32, 0.0, 1)
        return (x, src, dst, edge_type_200, edge_weight)
    x, src, dst, edge_type_200, edge_weight = _rec_inputs()

    def _L0_gnn_setup():
        import jax, jax.numpy as jnp
        import numpy as np
        N_NODES = 3125
        N_EDGES = 50000
        D = 64
        N_RELS = 200
        key = jax.random.key(seed)
        ks = jax.random.split(key, 8)
        h = jax.random.normal(ks[0], (N_NODES, D), dtype=jnp.float32)
        emb_rel = jax.random.normal(ks[1], (N_RELS, D), dtype=jnp.float32)
        loop_weight = jax.random.normal(ks[2], (D, D), dtype=jnp.float32) * 0.1
        attn_w1 = jax.random.normal(ks[3], (3 * D, D), dtype=jnp.float32) * 0.1
        attn_w2 = jax.random.normal(ks[4], (D, 1), dtype=jnp.float32) * 0.1
        src = jax.random.randint(ks[5], (N_EDGES,), 0, N_NODES, dtype=jnp.int64)
        dst = jax.random.randint(ks[6], (N_EDGES,), 0, N_NODES, dtype=jnp.int64)
        etype = jax.random.randint(ks[7], (N_EDGES,), 0, N_RELS, dtype=jnp.int64)
        return {'h': h, 'emb_rel': emb_rel, 'loop_weight': loop_weight, 'attn_w1': attn_w1, 'attn_w2': attn_w2, 'src': src, 'dst': dst, 'etype': etype}
    _L0_gnn_all = _L0_gnn_setup()
    _L0_gnn_in = {k: v for k, v in _L0_gnn_all.items() if k in ('emb_rel', 'loop_weight', 'attn_w1', 'attn_w2')}
    del _L0_gnn_all

    def _L1_gnn_setup():
        import jax, jax.numpy as jnp
        import numpy as np
        N = 3125
        E = 50000
        D_IN = 64
        D_OUT = 64
        key = jax.random.key(seed)
        k1, k2, k3, k4, k5, k6 = jax.random.split(key, 6)
        x = jax.random.normal(k1, (N, D_IN), dtype=jnp.float32)
        edge_index = jax.random.randint(k2, (2, E), 0, N, dtype=jnp.int64)
        s_msg = 1.0 / np.sqrt(D_IN)
        s_upd = 1.0 / np.sqrt(D_IN + D_OUT)
        W_msg = jax.random.uniform(k3, (D_IN, D_OUT), jnp.float32, -s_msg, s_msg)
        b_msg = jax.random.uniform(k4, (D_OUT,), jnp.float32, -s_msg, s_msg)
        W_upd = jax.random.uniform(k5, (D_IN + D_OUT, D_OUT), jnp.float32, -s_upd, s_upd)
        b_upd = jax.random.uniform(k6, (D_OUT,), jnp.float32, -s_upd, s_upd)
        return {'x': x, 'edge_index': edge_index, 'W_msg': W_msg, 'b_msg': b_msg, 'W_upd': W_upd, 'b_upd': b_upd}
    _L1_gnn_all = _L1_gnn_setup()
    _L1_gnn_in = {k: v for k, v in _L1_gnn_all.items() if k in ('W_msg', 'b_msg', 'W_upd', 'b_upd')}
    del _L1_gnn_all

    def _L2_gnn_setup():
        import jax, jax.numpy as jnp
        import numpy as np
        N_NODES = 3125
        N_EDGES = 50000
        DIM = 64
        LAYERS = 2
        key = jax.random.key(seed)
        k1, k2, k3, k4 = jax.random.split(key, 4)
        h = jax.random.normal(k1, (N_NODES, DIM), dtype=jnp.float32)
        w = jax.random.uniform(k2, (N_EDGES,), dtype=jnp.float32)
        src = jax.random.randint(k3, (N_EDGES,), 0, N_NODES, dtype=jnp.int32)
        dst = jax.random.randint(k4, (N_EDGES,), 0, N_NODES, dtype=jnp.int32)
        return {'h': h, 'w': w, 'src': src, 'dst': dst}
    _L2_gnn_all = _L2_gnn_setup()
    _L2_gnn_in = {k: v for k, v in _L2_gnn_all.items() if k in ()}
    del _L2_gnn_all

    def _L3_gnn_setup():
        import jax, jax.numpy as jnp
        import numpy as np
        N, E, D, H = (50000, 15625, 64, 8)
        LN_EPS = 1e-05
        SM_EPS = 1e-16
        SLOPE = 0.2

        def layer_norm(x, g, b):
            mu = jnp.mean(x, axis=-1, keepdims=True)
            var = jnp.mean((x - mu) ** 2, axis=-1, keepdims=True)
            return (x - mu) * jax.lax.rsqrt(var + LN_EPS) * g + b
        key = jax.random.key(seed)
        ks = jax.random.split(key, 12)
        glorot = lambda k, shape: jax.random.normal(k, shape, jnp.float32) * np.sqrt(2.0 / (shape[0] + shape[-1]))
        return {'x': jax.random.normal(ks[0], (N, D), jnp.float32), 'edge_index': jax.random.randint(ks[1], (2, E), 0, N, jnp.int64), 'W_att': glorot(ks[2], (D, H * D)), 'att_src': glorot(ks[3], (H, D)), 'att_dst': glorot(ks[4], (H, D)), 'bias_att': jnp.zeros((D,), jnp.float32), 'W1': glorot(ks[5], (D, 2 * D)), 'b1': jnp.zeros((2 * D,), jnp.float32), 'W2': glorot(ks[6], (2 * D, D)), 'b2': jnp.zeros((D,), jnp.float32), 'ln1_g': jnp.ones((D,), jnp.float32), 'ln1_b': jnp.zeros((D,), jnp.float32), 'ln2_g': jnp.ones((D,), jnp.float32), 'ln2_b': jnp.zeros((D,), jnp.float32)}
    _L3_gnn_all = _L3_gnn_setup()
    _L3_gnn_in = {k: v for k, v in _L3_gnn_all.items() if k in ('W_att', 'att_src', 'att_dst', 'bias_att', 'W1', 'b1', 'W2', 'b2', 'ln1_g', 'ln1_b', 'ln2_g', 'ln2_b')}
    del _L3_gnn_all
    return {'x': x, 'src': src, 'dst': dst, 'edge_type_200': edge_type_200, 'edge_weight': edge_weight, 'L0_gnn_emb_rel': _L0_gnn_in['emb_rel'], 'L0_gnn_loop_weight': _L0_gnn_in['loop_weight'], 'L0_gnn_attn_w1': _L0_gnn_in['attn_w1'], 'L0_gnn_attn_w2': _L0_gnn_in['attn_w2'], 'L1_gnn_W_msg': _L1_gnn_in['W_msg'], 'L1_gnn_b_msg': _L1_gnn_in['b_msg'], 'L1_gnn_W_upd': _L1_gnn_in['W_upd'], 'L1_gnn_b_upd': _L1_gnn_in['b_upd'], 'L3_gnn_W_att': _L3_gnn_in['W_att'], 'L3_gnn_att_src': _L3_gnn_in['att_src'], 'L3_gnn_att_dst': _L3_gnn_in['att_dst'], 'L3_gnn_bias_att': _L3_gnn_in['bias_att'], 'L3_gnn_W1': _L3_gnn_in['W1'], 'L3_gnn_b1': _L3_gnn_in['b1'], 'L3_gnn_W2': _L3_gnn_in['W2'], 'L3_gnn_b2': _L3_gnn_in['b2'], 'L3_gnn_ln1_g': _L3_gnn_in['ln1_g'], 'L3_gnn_ln1_b': _L3_gnn_in['ln1_b'], 'L3_gnn_ln2_g': _L3_gnn_in['ln2_g'], 'L3_gnn_ln2_b': _L3_gnn_in['ln2_b']}

def reference(x, src, dst, edge_type_200, edge_weight, L0_gnn_emb_rel, L0_gnn_loop_weight, L0_gnn_attn_w1, L0_gnn_attn_w2, L1_gnn_W_msg, L1_gnn_b_msg, L1_gnn_W_upd, L1_gnn_b_upd, L3_gnn_W_att, L3_gnn_att_src, L3_gnn_att_dst, L3_gnn_bias_att, L3_gnn_W1, L3_gnn_b1, L3_gnn_W2, L3_gnn_b2, L3_gnn_ln1_g, L3_gnn_ln1_b, L3_gnn_ln2_g, L3_gnn_ln2_b):
    import jax
    import jax.numpy as jnp

    def _L0_gnn_ref(h, emb_rel, loop_weight, attn_w1, attn_w2, src, dst, etype):
        import jax, jax.numpy as jnp
        import numpy as np
        N_NODES = 3125
        N_EDGES = 50000
        D = 64
        N_RELS = 200
        N = h.shape[0]
        loop = h @ loop_weight
        hs = h[src]
        hd = h[dst]
        r = emb_rel[etype]
        z = jnp.concatenate([hs, hd, r], axis=1)
        e = jax.nn.leaky_relu(z @ attn_w1 @ attn_w2, negative_slope=0.01)[:, 0]
        m = jax.ops.segment_max(e, dst, num_segments=N)
        ex = jnp.exp(e - m[dst])
        denom = jax.ops.segment_sum(ex, dst, num_segments=N)
        a = ex / denom[dst]
        agg = jax.ops.segment_sum(a[:, None] * hs, dst, num_segments=N)
        deg = jax.ops.segment_sum(jnp.ones_like(e), dst, num_segments=N)
        h_new = jnp.where(deg[:, None] > 0, agg, h)
        return jax.nn.relu(h_new + loop)

    def _L1_gnn_ref(x, edge_index, W_msg, b_msg, W_upd, b_upd):
        import jax, jax.numpy as jnp
        import numpy as np
        N = 3125
        E = 50000
        D_IN = 64
        D_OUT = 64
        row, col = (edge_index[0], edge_index[1])
        messages = x[col] @ W_msg + b_msg
        aggr = jax.ops.segment_sum(messages, row, num_segments=x.shape[0])
        h = jnp.concatenate([x, aggr], axis=1)
        return jax.nn.relu(h @ W_upd + b_upd)

    def _L2_gnn_ref(h, w, src, dst):
        import jax, jax.numpy as jnp
        import numpy as np
        N_NODES = 3125
        N_EDGES = 50000
        DIM = 64
        LAYERS = 2
        N = h.shape[0]
        deg = jnp.maximum(jax.ops.segment_sum(w, dst, num_segments=N), 1.0)
        norm = deg[:, None] ** (-0.5)
        embs = [h]
        for _ in range(LAYERS):
            h_norm = h * norm
            m = h_norm[src] * w[:, None]
            neigh_sum = jax.ops.segment_sum(m, dst, num_segments=N)
            h = neigh_sum * norm
            embs.append(h)
        return jnp.mean(jnp.stack(embs, axis=1), axis=1)

    def _L3_gnn_ref(x, edge_index, W_att, att_src, att_dst, bias_att, W1, b1, W2, b2, ln1_g, ln1_b, ln2_g, ln2_b):
        import jax, jax.numpy as jnp
        import numpy as np
        N, E, D, H = (50000, 15625, 64, 8)
        LN_EPS = 1e-05
        SM_EPS = 1e-16
        SLOPE = 0.2

        def layer_norm(x, g, b):
            mu = jnp.mean(x, axis=-1, keepdims=True)
            var = jnp.mean((x - mu) ** 2, axis=-1, keepdims=True)
            return (x - mu) * jax.lax.rsqrt(var + LN_EPS) * g + b
        n = x.shape[0]
        h = (x @ W_att).reshape(n, H, D)
        a_src = jnp.einsum('nhc,hc->nh', h, att_src)
        a_dst = jnp.einsum('nhc,hc->nh', h, att_dst)
        loops = jnp.arange(n, dtype=edge_index.dtype)
        src = jnp.concatenate([edge_index[0], loops])
        dst = jnp.concatenate([edge_index[1], loops])
        e = a_src[src] + a_dst[dst]
        e = jnp.where(e > 0, e, SLOPE * e)
        m = jax.ops.segment_max(e, dst, num_segments=n)
        e = jnp.exp(e - m[dst])
        s = jax.ops.segment_sum(e, dst, num_segments=n)
        alpha = e / (s[dst] + SM_EPS)
        msg = alpha[:, :, None] * h[src]
        out = jax.ops.segment_sum(msg, dst, num_segments=n)
        att_out = out.mean(axis=1) + bias_att
        x1 = layer_norm(att_out + x, ln1_g, ln1_b)
        ff = jax.nn.relu(x1 @ W1 + b1) @ W2 + b2
        return layer_norm(ff + x1, ln2_g, ln2_b)
    edge_index = jnp.stack([src, dst])
    h = jnp.maximum(_layernorm(x, axis=-1), 0.0)
    x = x + _L0_gnn_ref(h, L0_gnn_emb_rel, L0_gnn_loop_weight, L0_gnn_attn_w1, L0_gnn_attn_w2, src, dst, edge_type_200)
    h = jnp.maximum(_layernorm(x, axis=-1), 0.0)
    x = x + _L1_gnn_ref(h, edge_index, L1_gnn_W_msg, L1_gnn_b_msg, L1_gnn_W_upd, L1_gnn_b_upd)
    h = jnp.maximum(_layernorm(x, axis=-1), 0.0)
    x = x + _L2_gnn_ref(h, edge_weight, src, dst)
    h = jnp.maximum(_layernorm(x, axis=-1), 0.0)
    x = x + _L3_gnn_ref(h, edge_index, L3_gnn_W_att, L3_gnn_att_src, L3_gnn_att_dst, L3_gnn_bias_att, L3_gnn_W1, L3_gnn_b1, L3_gnn_W2, L3_gnn_b2, L3_gnn_ln1_g, L3_gnn_ln1_b, L3_gnn_ln2_g, L3_gnn_ln2_b)
    return x

_drawn_inputs = setup_inputs


def setup_inputs(seed=0):
    import zlib

    import numpy as np

    out = dict(_drawn_inputs(seed))
    spreads = {'L3_gnn_bias_att': (0.0, 0.295),
     'L3_gnn_b1': (0.0, 0.442),
     'L3_gnn_b2': (0.0, 0.422),
     'L3_gnn_ln1_g': (1.0, 0.2),
     'L3_gnn_ln1_b': (0.0, 0.332),
     'L3_gnn_ln2_g': (1.0, 0.2),
     'L3_gnn_ln2_b': (0.0, 0.387)}
    factors = {'edge_weight': 59.205,
     'L1_gnn_b_upd': 3.081,
     'L3_gnn_att_src': 64.0,
     'L3_gnn_att_dst': 64.0,
     'L0_gnn_emb_rel': 2.676}
    for name, (base, spread) in spreads.items():
        noise = np.random.default_rng([zlib.crc32(name.encode()), seed]).standard_normal(out[name].shape)
        drawn = base * np.exp(spread * noise) if base else spread * noise
        out[name] = jnp.asarray(drawn.astype(out[name].dtype))
    for name, factor in factors.items():
        out[name] = (out[name] * factor).astype(out[name].dtype)
    return out
```

```python
from contextlib import ExitStack

import concourse.bass as bass
from concourse import mybir

ALU = mybir.AluOpType
ACT = mybir.ActivationFunctionType
AX_X = mybir.AxisListType.X
F32 = mybir.dt.float32
BF16 = mybir.dt.bfloat16
I32 = mybir.dt.int32
I16 = mybir.dt.int16

P = 128
RING = 16
HALF = RING // 2
BIG = 1.0e38
LN_EPS = 1e-5
SM_EPS = 1e-16


def free(ap, dims, offset=0):
    return bass.AP(ap.tensor, ap.offset + offset, [list(ap.ap[0]), *[list(d) for d in dims]])


def rows_on_all(dram, parts):
    n = 1
    for s in dram.shape:
        n *= s
    return bass.AP(dram.tensor, dram.offset, [[0, parts], [1, n]])


def gnn_four_layers(
    nc, x, src, dst, etype, weight, emb_rel, loop_weight, attn_w1, attn_w2, W_msg, b_msg, W_upd, b_upd,
    W_att, att_src, att_dst, bias_att, W1, b1, W2, b2, ln1_g, ln1_b, ln2_g, ln2_b, out,
):
    N, D = x.shape
    E = src.shape[0]
    RELS = emb_rel.shape[0]
    H = att_src.shape[0]
    NP = 125
    NB = N // NP
    assert NB * NP == N and D == 64
    C = -(-E // (P * RING)) * RING
    EP = P * C
    FULL = E // C
    REST = E - FULL * C
    assert FULL == P - 1 and C * P * RING >= E
    TILES = -(-E // P)
    K = -(-(TILES + NB - 1) // RING) * RING
    KG = -(-K // P)
    KP = KG * P
    LIN_ITERS = C // RING
    AGG_ITERS = K // RING
    PAD_TILE = C - 1
    assert TILES <= PAD_TILE
    OUT_OF_RANGE = 2.0 * EP
    HD = H * D
    BANK = 512
    PERB = 4

    ctx = ExitStack()
    with ctx:
        def sb(name, shape, dt=F32):
            return ctx.enter_context(nc.sbuf_tensor(name, shape, dt))

        def sem(name):
            return ctx.enter_context(nc.semaphore(name))

        def dram(name, shape, dt=F32):
            return nc.dram_tensor(name, shape, dt).ap()

        d_edges = dram("d_edges", (EP, 3))
        d_pair = dram("d_pair", (N * RELS, 1))
        d_tab = [dram(f"d_tab{i}", (N, D)) for i in range(4)]
        d_y = dram("d_y", (N, HD))
        d_as = dram("d_as", (N, H))
        d_max0, d_sum0 = dram("d_max0", (EP, 1)), dram("d_sum0", (EP, 1))
        d_max3, d_sum3 = dram("d_max3", (EP, H)), dram("d_sum3", (EP, H))
        d_fa0, d_fb0 = dram("d_fa0", (EP, 2)), dram("d_fb0", (EP, 1))
        d_fa3, d_fb3 = dram("d_fa3", (EP, 2 * H)), dram("d_fb3", (EP, H))
        d_al0, d_al3 = dram("d_al0", (EP, 1)), dram("d_al3", (EP, H))

        PS = ctx.enter_context(nc.psum_tensor("PS", [P, 8 * BANK], F32))

        ident = sb("ident", [P, P])
        ones = sb("ones", [P, P])
        tri = sb("tri", [NP, NP])
        iota_row = sb("iota_row", [P, KP])
        iota_bf = sb("iota_bf", [P, NP + 1], BF16)
        kg_i = sb("kg_i", [P, KG], I32)
        zero_bf = sb("zero_bf", [P, BANK], BF16)

        w1t_in = sb("w1t_in", [D, 3, D])
        w2_col = sb("w2_col", [D, 1])
        emb = sb("emb", [RELS // 2, 2, D])
        w1T = sb("w1T", [D, 3 * D])
        embT = sb("embT", [D, RELS])
        vv = sb("vv", [D, 3])
        vr_b = sb("vr_b", [D, P])
        rhs0 = sb("rhs0", [D, D + 2])
        wm = sb("wm", [D, D])
        wu_top = sb("wu_top", [D, D])
        wu_bot2 = sb("wu_bot2", [2 * D, D])
        watt = sb("watt", [D, HD])
        w_asd = sb("w_asd", [D, 2 * H])
        w1_sb = sb("w1_sb", [D, 2 * D])
        b1_col = sb("b1_col", [2 * D, 1])
        w2_sb = sb("w2_sb", [2 * D, D])
        vec = sb("vec", [P, 8, D])
        BM, BU, BA, B2, G1, E1, G2, E2 = range(8)

        big = sb("big", [P, NB * HD])
        ints = big[:, 0:3 * C].bitcast(I32)
        dst_i, prev_i, src_i = (ints[:, j * C:(j + 1) * C] for j in range(3))
        ety_i = big[:, 3 * C:4 * C].bitcast(I32)
        w_lin = big[:, 4 * C:5 * C]
        edge_lin = free(big[:, 5 * C:5 * C + 1], [[3, C], [1, 3]])
        junk = sb("junk", [P, max(C, KP)])
        iota_i = junk[:, 0:KP].bitcast(I32)

        notst = sb("notst", [P, C])
        negst = sb("negst", [P, C])
        cf_sum = sb("cf_sum", [2 * H, P])
        cf_max = sb("cf_max", [2 * H, P])
        chain_in = sb("chain_in", [P, 2 * H])
        idx_pair = sb("idx_pair", [P, C + RING], I32)
        idx_src = sb("idx_src", [P, C + RING], I32)
        cnt = sb("cnt", [P, NB + 1])
        R = sb("R", [P, NB + 1])
        small = sb("small", [P, 8, NB + 1])
        small_i = sb("small_i", [P, 2, NB + 1], I32)
        tk = sb("tk", [P, KG])
        tk2 = sb("tk2", [P, KG])
        tk_i = sb("tk_i", [P, KG], I32)
        bk = sb("bk", [P, KP])
        bk_i = sb("bk_i", [1, KP], I32)

        dstl = sb("dstl", [P, KP])
        srcm = sb("srcm", [P, KP])
        wk = sb("wk", [P, KP])
        idx_src_k = sb("idx_src_k", [P, KP + RING], I32)
        idx_dst_k = sb("idx_dst_k", [P, KP + RING], I32)
        w4 = sb("w4", [P, KP, 4], BF16)
        alpha0 = bk
        qa = sb("qa", [P, KP * H])
        zrow = qa[:, 0:C]
        iota_n = qa[:, H * C - (N + 1) // 2:H * C].bitcast(I16)
        idx_ring = sb("idx_ring", [P, RING], I32)
        ring = sb("ring", [P, RING, D])
        yring = big[:, 0:RING // 2 * HD].rearrange("p (s m) -> p s m", m=HD)
        s_ring = sb("s_ring", [P, RING, NP + 1])
        s_bf = free(s_ring[:, 0, 0:1].bitcast(BF16), [[2 * (NP + 1), RING], [1, NP + 1]])
        PR = 2
        prod = sb("prod", [P, PR, HD])

        split_t = free(w4[:, 0, 0:1], [[3 * D, RING], [1, 3 * D]])
        fres = big[:, 7168:7168 + RING * D].rearrange("p (s f) -> p s f", f=D)
        OHS = 4
        oh_all = big[:, 0:OHS * (N + 3) // 2].bitcast(BF16)

        def split(s):
            return split_t[:, s, :]

        def parts(lo, hi, j):
            return split_t[:, lo:hi, j * D:(j + 1) * D]

        def onehot(s):
            return oh_all[:, (s % OHS) * (N + 3):(s % OHS) * (N + 3) + N + 1]

        att_b = big[0:D, HD:3 * HD].rearrange("p (j m) -> p j m", j=2)

        X = sb("X", [NP, NB, D])
        Hn = sb("Hn", [NP, NB, D])
        T1 = sb("T1", [NP, NB, D])
        T2 = sb("T2", [NP, NB, D])
        HT = sb("HT", [D, NB, NP])
        st = sb("st", [NP, 4, NB])
        deg = sb("deg", [NP, NB])
        norm = sb("norm", [NP, NB])
        start_i = sb("start_i", [NP, NB], I32)
        last_i = sb("last_i", [NP, NB], I32)
        nfl = sb("nfl", [NP, 4, NB])
        asd = sb("asd", [NP, NB, 2 * H])
        nmx = sb("nmx", [NP, NB, H])
        nfill = sb("nfill", [NP, NB, 2 * H])
        nself = sb("nself", [NP, NB, H])
        nden = sb("nden", [NP, NB, H])
        ends = sb("ends", [P, 2 * H])
        carry_row = sb("carry_row", [2 * H, P + 1])
        carry = sb("carry", [P, 2 * H])

        names = """consts preinc pads edges_in w_in weights_in x_in vecs_in zero_ready fills_zero
            wtr wtr_sb vproj vv_ready vrb_ready h_ready ht_psum ht_sb node_mm node_sb asd_sb
            pair_ready pair_out edges_ready edges_out cnt_ready cnt_sum tk_ready rows_in rows_tr rows_sb
            steps_ready hist_s hist_used hist_done tri_in tri_done idx_ready
            staged ring_used s_ready prod_done lin_done agg_zero agg_done
            ends_ready ends_tr carry_in carry_tr chain_ready chain_tr
            scan_ready scan_out nodes_in fill_ready fill_out fill_in alpha_ready alpha_out
            tab_ready tab_out dve halves_begun ln_var ln_root x_done out_done y_bank y_sb y_out y_back watt_in
            wasd_ready ff1 ff1_sb exp_in exp_done oh_ready a_sb split_dve nmx_ready""".split()
        S = {n: sem(n) for n in names}
        slot = [sem(f"slot{i}") for i in range(RING)]

        PASSES = [("pair", LIN_ITERS), ("l0", AGG_ITERS), ("l1", AGG_ITERS), ("l2a", AGG_ITERS),
                  ("l2b", AGG_ITERS), ("as", LIN_ITERS), ("l3", AGG_ITERS)]
        ITERS = dict(PASSES)
        BASE = {n: sum(k for _, k in PASSES[:i]) for i, (n, _) in enumerate(PASSES)}
        STAGE_BASE = {n: 2 * (BASE[n] + i) for i, (n, _) in enumerate(PASSES)}
        S_BASE = {n: K * i for i, n in enumerate(["l0", "l2a", "l2b", "l3"])}

        ROW_WIDTH = [3, 1, H]
        ROW_UNITS = [-(-KG * w // PERB) for w in ROW_WIDTH]
        ROW_BASE = [0, ROW_UNITS[0], ROW_UNITS[0] + ROW_UNITS[1]]
        steps3 = big[:, 6 * KP:9 * KP]

        def rows_buf(turn):
            w = ROW_WIDTH[turn]
            at = big.shape[1] - KG * P * w if turn == 0 else 0
            return big[:, at:at + KG * P * w]

        def rows_dst(turn):
            return [steps3, alpha0[:, :], qa[:, :]][turn]

        def bank(j, parts, cols, at=0):
            return PS[0:parts, j * BANK + at:j * BANK + at + cols]

        def agg_psum():
            return free(PS[0:NP, 0:1], [[D, NB], [1, D]])

        def packed(t, w):
            return free(t[0:NP, 0, 0:1], [[w, NB], [1, w]])

        def col(buf, j, w):
            return free(buf[:, 0:1], [[w, C]], j)

        block = ctx.enter_context(nc.Block())

        @block.sync
        def _(sp):
            src1, dst1, ety1, wt1 = (a.rearrange("(o e) -> o e", o=1) for a in (src, dst, etype, weight))
            sp.wait_ge(S["pads"], 1)
            for sb_t, dr in ((dst_i, dst1), (src_i, src1), (ety_i, ety1), (w_lin, wt1)):
                sp.dma_start(sb_t[0:FULL, :], dr[0, 0:FULL * C].rearrange("(p c) -> p c", c=C)).then_inc(S["edges_in"], 16)
                sp.dma_start(sb_t[FULL:P, 0:REST], dr[0:1, FULL * C:E]).then_inc(S["edges_in"], 16)
            sp.dma_start(prev_i[0:1, 1:C], dst1[0:1, 0:C - 1]).then_inc(S["edges_in"], 16)
            sp.dma_start(prev_i[1:FULL, :], dst1[0, C - 1:FULL * C - 1].rearrange("(p c) -> p c", c=C)).then_inc(S["edges_in"], 16)
            sp.dma_start(prev_i[FULL:P, 0:REST + 1], dst1[0:1, FULL * C - 1:E]).then_inc(S["edges_in"], 16)
            sp.dma_start(X[:], x.rearrange("(b p) f -> p b f", p=NP)).then_inc(S["x_in"], 16)
            for t, d in (
                (w1t_in[:], attn_w1.rearrange("(a i) j -> i a j", a=3)), (w2_col[:], attn_w2),
                (emb[:], emb_rel.rearrange("(g p) d -> p g d", g=2)), (rhs0[:, 0:D], loop_weight),
                (wm[:], W_msg), (wu_top[:], W_upd[0:D, :]), (wu_bot2[0:D, :], W_upd[D:2 * D, :]),
                (wu_bot2[D:2 * D, :], W_upd[D:2 * D, :]), (watt[:], W_att), (w1_sb[:], W1),
                (b1_col[:], b1.rearrange("(p o) -> p o", o=1)), (w2_sb[:], W2),
            ):
                sp.dma_start(t, d).then_inc(S["weights_in"], 16)
            for j, v in enumerate((b_msg, b_upd, bias_att, b2, ln1_g, ln1_b, ln2_g, ln2_b)):
                sp.dma_start(vec[:, j, :], rows_on_all(v, P)).then_inc(S["vecs_in"], 16)
            sp.wait_ge(S["edges_ready"], 1)
            sp.dma_start(d_edges.rearrange("(p c) k -> p (c k)", p=P), big[:, 5 * C:8 * C]).then_inc(S["edges_out"], 16)
            sp.wait_ge(S["zero_ready"], 1)
            for d in (d_fa0, d_fb0, d_fa3, d_fb3):
                flat = d.rearrange("e k -> (e k)")
                for j in range(d.shape[1]):
                    sp.dma_start(flat[j * EP:(j + 1) * EP].rearrange("(p c) -> p c", p=P), zrow[:]).then_inc(S["fills_zero"], 16)
            sp.wait_ge(S["pair_ready"], 1)
            sp.dma_start(d_pair.rearrange("(b p r) o -> p b (r o)", b=NB, p=NP),
                         free(big[0:NP, 0:1], [[RELS, NB], [1, RELS]])).then_inc(S["pair_out"], 16)
            sp.dma_start(d_tab[0].rearrange("(b p) f -> p b f", p=NP), Hn[:]).then_inc(S["tab_out"], 16)

            def softmax_dmas(turn, nh, lin, d_max, d_sum, d_fa, d_fb, d_al):
                w = nh * C
                sp.wait_ge(S["scan_ready"], 2 * turn + 1)
                sp.dma_start(d_max.rearrange("(p c) k -> p (c k)", p=P), lin).then_inc(S["scan_out"], 16)
                sp.wait_ge(S["fill_out"], 16 * NB * (2 * turn + 1))
                sp.dma_start(big[:, 0:2 * w], d_fa.rearrange("(p c) k -> p (c k)", p=P)).then_inc(S["fill_in"], 16)
                sp.wait_ge(S["scan_ready"], 2 * turn + 2)
                sp.dma_start(d_sum.rearrange("(p c) k -> p (c k)", p=P), big[:, 0:w]).then_inc(S["scan_out"], 16)
                sp.wait_ge(S["fill_out"], 16 * NB * (2 * turn + 2))
                sp.dma_start(big[:, w:2 * w], d_fb.rearrange("(p c) k -> p (c k)", p=P)).then_inc(S["fill_in"], 16)
                sp.wait_ge(S["alpha_ready"], turn + 1)
                sp.dma_start(d_al.rearrange("(p c) k -> p (c k)", p=P), qa[:, 0:w]).then_inc(S["alpha_out"], 16)

            softmax_dmas(0, 1, big[:, 0:C], d_max0, d_sum0, d_fa0, d_fb0, d_al0)
            for j in (1, 2, 3):
                sp.wait_ge(S["tab_ready"], j)
                sp.dma_start(d_tab[j].rearrange("(b p) f -> p b f", p=NP), T1[:]).then_inc(S["tab_out"], 16)
            for j, v in enumerate((att_src, att_dst)):
                sp.dma_start(att_b[:, j, :], rows_on_all(v, D)).then_inc(S["watt_in"], 16)
            sp.wait_ge(S["asd_sb"], 1)
            sp.dma_start(d_as.rearrange("(b p) h -> p b h", p=NP), asd[:, :, 0:H]).then_inc(S["y_out"], 16)
            sp.wait_ge(S["y_sb"], NB)
            y_dram = d_y.rearrange("(b p) m -> p b m", p=NP)
            sp.dma_start(y_dram, big[0:NP, :].rearrange("p (b m) -> p b m", b=NB)).then_inc(S["y_out"], 16)
            softmax_dmas(1, H, big[:, 0:H * C], d_max3, d_sum3, d_fa3, d_fb3, d_al3)
            sp.wait_ge(S["ring_used"], RING * (BASE["l3"] + AGG_ITERS + 1))
            sp.dma_start(big[0:NP, :].rearrange("p (b m) -> p b m", b=NB), y_dram).then_inc(S["y_back"], 16)
            sp.wait_ge(S["x_done"], 1)
            sp.dma_start(out.rearrange("(b p) f -> p b f", p=NP), X[:]).then_inc(S["out_done"], 16)
            sp.wait_ge(S["out_done"], 16)

        @block.gpsimd
        def _(pool):
            nc.gpsimd.memset(dst_i[:, :], E)
            nc.gpsimd.memset(prev_i[:, :], E)
            nc.gpsimd.memset(src_i[:, :], 0)
            nc.gpsimd.memset(ety_i[:, :], 0)
            nc.gpsimd.memset(w_lin[:, :], 0.0).then_inc(S["pads"], 1)
            nc.gpsimd.memset(zrow[:], 0.0).then_inc(S["zero_ready"], 1)
            nc.gpsimd.memset(zero_bf[:], 0.0)
            nc.gpsimd.memset(ones[:], 1.0)
            nc.gpsimd.memset(ident[:], 0.0)
            nc.gpsimd.memset(tri[:], 1.0).then_inc(S["preinc"], 1)
            pool.wait_ge(S["preinc"], 1)
            nc.gpsimd.affine_select(out=ident[:], in_=ident[:], compare_op=ALU.not_equal, fill=1.0,
                                    base=0, pattern=[[-1, P]], channel_multiplier=1)
            nc.gpsimd.affine_select(out=tri[:], in_=tri[:], compare_op=ALU.is_gt, fill=0.0,
                                    base=0, pattern=[[1, NP]], channel_multiplier=-1)
            nc.gpsimd.iota(iota_n, [[1, N + 1]], base=0, channel_multiplier=0, allow_small_or_imprecise_dtypes=True)
            nc.gpsimd.iota(kg_i[:], [[P, KG]], base=0, channel_multiplier=1)
            nc.gpsimd.iota(iota_i[:], [[1, KP]], base=0, channel_multiplier=0).then_inc(S["consts"], 1)
            pool.sem_inc(S["ring_used"], RING)
            pool.sem_inc(S["hist_used"], RING)

            def gather_pass(name, table, into, depth=RING):
                base, sbase = BASE[name], STAGE_BASE[name]
                with pool.Fori(0, ITERS[name]) as i:
                    for h in range(2):
                        pool.wait_ge(S["staged"], 2 * i + (sbase + h + 1))
                        if depth == RING:
                            pool.wait_ge(S["ring_used"], RING * i + (RING * base + HALF * (h + 1)))
                        pool.sem_inc(S["halves_begun"], 1)
                        for s in range(HALF * h, HALF * h + HALF):
                            if depth < RING:
                                pool.wait_ge(S["ring_used"], RING * i + (RING * base + s + 1 + RING - depth))
                                pool.sem_inc(S["halves_begun"], 1)
                            pool.indirect_dma_start(
                                into[:, s % depth, :], None, table,
                                bass.IndirectOffsetOnAxis(ap=idx_ring[:, s:s + 1], axis=0)).then_inc(slot[s], 16)

            def row_gather(turn, d):
                w = ROW_WIDTH[turn]
                buf = rows_buf(turn)
                table = d.rearrange("(t e) k -> t (e k)", e=P)
                for g in range(KG):
                    pool.indirect_dma_start(buf[:, g * P * w:(g + 1) * P * w], None, table,
                                            bass.IndirectOffsetOnAxis(ap=tk_i[:, g:g + 1], axis=0)).then_inc(S["rows_in"], 16)

            def from_segments(table, into, w):
                into = packed(into, w)
                for b in range(NB):
                    pool.indirect_dma_start(into[:, b, :], None, table,
                                            bass.IndirectOffsetOnAxis(ap=last_i[:, b:b + 1], axis=0),
                                            bounds_check=EP - 1, oob_is_err=False).then_inc(S["nodes_in"], 16)

            def to_segments(table, w):
                vals = packed(nfill, w)
                for b in range(NB):
                    pool.indirect_dma_start(table, bass.IndirectOffsetOnAxis(ap=start_i[:, b:b + 1], axis=0),
                                            vals[:, b, :], None,
                                            bounds_check=EP - 1, oob_is_err=False).then_inc(S["fill_out"], 16)

            def softmax_nodes(turn, nh, d_max, d_sum, d_fa, d_fb, d_al):
                pool.wait_ge(S["nmx_ready"], turn + 1)
                pool.wait_ge(S["scan_out"], 16 * (2 * turn + 1))
                from_segments(d_max, nmx, nh)
                pool.wait_ge(S["fill_ready"], 2 * turn + 1)
                to_segments(d_fa, 2 * nh)
                pool.wait_ge(S["scan_out"], 16 * (2 * turn + 2))
                from_segments(d_sum, nden, nh)
                pool.wait_ge(S["fill_ready"], 2 * turn + 2)
                to_segments(d_fb, nh)
                pool.wait_ge(S["alpha_out"], 16 * (turn + 1))
                row_gather(turn + 1, d_al)

            pool.wait_ge(S["tk_ready"], 1)
            pool.wait_ge(S["edges_out"], 16)
            row_gather(0, d_edges)
            pool.wait_ge(S["pair_out"], 16)
            gather_pass("pair", d_pair, free(ring[:, 0, 0:1], [[1, RING], [1, 1]]))
            pool.wait_ge(S["idx_ready"], 1)
            pool.wait_ge(S["fills_zero"], 16 * (2 + 1 + 2 * H + H))
            softmax_nodes(0, 1, d_max0, d_sum0, d_fa0, d_fb0, d_al0)
            pool.wait_ge(S["tab_out"], 16)
            gather_pass("l0", d_tab[0], ring)
            for name, j in (("l1", 1), ("l2a", 2), ("l2b", 3)):
                pool.wait_ge(S["tab_out"], 16 * (j + 1))
                gather_pass(name, d_tab[j], ring)
            pool.wait_ge(S["y_out"], 32)
            gather_pass("as", d_as, free(ring[:, 0, 0:1], [[H, RING], [1, H]]))
            softmax_nodes(1, H, d_max3, d_sum3, d_fa3, d_fb3, d_al3)
            gather_pass("l3", d_y, yring, depth=RING // 2)

        @block.scalar
        def _(act):
            def root(turn):
                act.wait_ge(S["ln_var"], turn + 1)
                nc.scalar.activation(st[:, 2, :], st[:, 1, :], ACT.Sqrt).then_inc(S["ln_root"], 1)

            def turned(turn):
                act.wait_ge(S["ht_psum"], turn + 1)
                for j in range(-(-NB // PERB)):
                    n = min(PERB, NB - PERB * j)
                    last = nc.scalar.activation(
                        HT[:, PERB * j:PERB * j + n, :],
                        bank(j, D, PERB * P).rearrange("p (n c) -> p n c", c=P)[:, 0:n, 0:NP], ACT.Copy)
                last.then_inc(S["ht_sb"], 1)

            def stage(idx, i, h):
                nc.scalar.activation(idx_ring[:, HALF * h:HALF * h + HALF],
                                     idx[:, bass.ds(RING * i + HALF * h, HALF)], ACT.Copy).then_inc(S["staged"], 1)

            def index_pass(name, idx, width=None):
                base = BASE[name]
                act.wait_ge(S["staged"], STAGE_BASE[name])
                for h in range(2):
                    stage(idx, 0, h)
                with act.Fori(0, ITERS[name]) as i:
                    for h in range(2):
                        for s in range(HALF * h, HALF * h + HALF):
                            act.wait_ge(slot[s], 16 * i + 16 * (base + 1))
                        if width:
                            nc.scalar.activation(
                                qa[:, bass.ds((RING * i + HALF * h) * width, HALF * width)],
                                free(ring[:, 0, 0:1], [[1, HALF * width]], HALF * width * h),
                                ACT.Copy).then_inc(S["ring_used"], HALF)
                        nc.scalar.activation(idx_ring[:, HALF * h:HALF * h + HALF],
                                             idx[:, bass.ds(RING * i + (RING + HALF * h), HALF)],
                                             ACT.Copy).then_inc(S["staged"], 1)

            def rows_out(turn):
                w, dst = ROW_WIDTH[turn], rows_dst(turn)
                for u in range(ROW_UNITS[turn]):
                    act.wait_ge(S["rows_tr"], ROW_BASE[turn] + u + 1)
                    n = min(PERB, KG * w - PERB * u) * P
                    nc.scalar.activation(dst[:, u * BANK:u * BANK + n], bank(u % 8, P, n), ACT.Copy).then_inc(S["rows_sb"], 1)

            root(0)
            turned(0)
            rows_out(0)
            act.wait_ge(S["edges_ready"], 1)
            act.wait_ge(S["fills_zero"], 16 * (2 + 1 + 2 * H + H))
            index_pass("pair", idx_pair, 1)
            act.wait_ge(S["exp_in"], 1)
            nc.scalar.activation(qa[:, 0:C], qa[:, 0:C], ACT.Exp).then_inc(S["exp_done"], 1)
            rows_out(1)
            act.wait_ge(S["steps_ready"], 1)
            index_pass("l0", idx_src_k)
            root(1)
            turned(1)
            index_pass("l1", idx_dst_k)
            root(2)
            root(3)
            index_pass("l2a", idx_src_k)
            index_pass("l2b", idx_src_k)
            root(4)
            turned(2)
            for b in range(NB):
                act.wait_ge(S["y_bank"], b + 1)
                nc.scalar.activation(big[0:NP, b * HD:(b + 1) * HD], bank(b % 7, NP, HD), ACT.Copy).then_inc(S["y_sb"], 1)
            index_pass("as", idx_src, H)
            act.wait_ge(S["exp_in"], 2)
            nc.scalar.activation(packed(nself, H), packed(nself, H), ACT.Exp)
            nc.scalar.activation(qa[:, 0:H * C], qa[:, 0:H * C], ACT.Exp).then_inc(S["exp_done"], 1)
            rows_out(2)
            index_pass("l3", idx_src_k)
            root(5)
            turned(3)
            act.wait_ge(S["ff1"], 1)
            for j in range(-(-N // 500)):
                n = min(500, N - 500 * j)
                last = nc.scalar.activation(big[:, 500 * j:500 * j + n], bank(j, P, n), ACT.Relu, bias=b1_col[:, 0:1])
            last.then_inc(S["ff1_sb"], 1)
            root(6)

        @block.tensor
        def _(pe):
            def turn_nodes(turn):
                pe.wait_ge(S["h_ready"], turn + 1)
                for b in range(NB):
                    last = nc.tensor.transpose(bank(b // PERB, D, NP, (b % PERB) * P), Hn[:, b, :], ident[0:NP, 0:NP])
                last.then_inc(S["ht_psum"], 1)
                pe.wait_ge(S["ht_sb"], turn + 1)

            def turn_rows(turn):
                w, buf = ROW_WIDTH[turn], rows_buf(turn)
                pe.wait_ge(S["rows_in"], 16 * KG * (turn + 1))
                for u in range(ROW_UNITS[turn]):
                    if u >= 8:
                        pe.wait_ge(S["rows_sb"], ROW_BASE[turn] + u - 7)
                    for q in range(PERB * u, min(PERB * u + PERB, KG * w)):
                        h, g = q // KG, q % KG
                        last = nc.tensor.transpose(bank(u % 8, P, P, (q % PERB) * P),
                                                   free(buf[:, 0:1], [[w, P]], g * P * w + h), ident[:])
                    last.then_inc(S["rows_tr"], 1)

            def zero_banks(first, n, parts=NP):
                for j in range(first, first + n):
                    nc.tensor.matmul(bank(j, parts, BANK), zero_bf[:, 0:parts], zero_bf[:], start=True, stop=True)

            def load_blocks(i):
                return nc.values_load_multi_w_load_instructions(
                    bk_i[0:1, bass.ds(RING * i, RING)], engines=[mybir.EngineType.PE], min_val=0, max_val=NB - 1,
                    skip_runtime_bounds_check_because="a step's block is a count of at most NB - 1 offsets")[1]

            def agg_pass(name):
                base, ob = BASE[name], S_BASE[name]
                zero_banks(0, 4)
                with pe.Fori(0, AGG_ITERS) as i:
                    blocks = load_blocks(i)
                    for s in range(RING):
                        pe.wait_ge(slot[s], 16 * i + 16 * (base + 1))
                        pe.wait_ge(S["s_ready"], RING * i + (ob + s + 1))
                        if name == "l3":
                            for j in range(4):
                                mm = nc.tensor.matmul(PS[0:NP, bass.ds(blocks[s] * D, D)], s_ring[:, s, 0:NP],
                                                      prod[:, s % PR, j * D:(j + 1) * D], start=False, stop=False, skip_group_check=True)
                        else:
                            mm = nc.tensor.matmul(PS[0:NP, bass.ds(blocks[s] * D, D)], s_ring[:, s, 0:NP],
                                                  ring[:, s, :], start=False, stop=False, skip_group_check=True)
                        mm.then_inc(S["ring_used"], 1)

            pe.wait_ge(S["consts"], 1)
            pe.wait_ge(S["cnt_ready"], 1)
            nc.tensor.transpose(bank(4, 2 * H, P), chain_in[:], ident[:])
            nc.tensor.matmul(bank(3, P, NB + 1), ones[:], cnt[:], start=True, stop=True).then_inc(S["chain_tr"], 1)
            pe.wait_ge(S["weights_in"], 16 * 12)
            for j in range(3):
                nc.tensor.transpose(bank(0, D, D, j * D), w1t_in[:, j, :], ident[0:D, 0:D])
            for g in range(2):
                mm = nc.tensor.transpose(bank(1, D, RELS // 2, g * RELS // 2), emb[:, g, :], ident[0:RELS // 2, 0:RELS // 2])
            mm.then_inc(S["wtr"], 1)
            pe.wait_ge(S["wtr_sb"], 1)
            for j in range(3):
                mm = nc.tensor.matmul(bank(2, D, 1, j), w1T[:, j * D:(j + 1) * D], w2_col[:], start=True, stop=True)
            mm.then_inc(S["vproj"], 1)
            turn_nodes(0)
            nc.tensor.matmul(bank(7, NP, RELS), vr_b[:, 0:NP], embT[:], start=True, stop=True)
            for b in range(NB):
                mm = nc.tensor.matmul(bank(b // PERB, NP, D + 2, (b % PERB) * P), HT[:, b, :], rhs0[:], start=True, stop=True)
            mm.then_inc(S["node_mm"], 1)
            pe.wait_ge(S["pair_ready"], 1)
            turn_rows(0)
            pe.wait_ge(S["rows_sb"], ROW_UNITS[0])
            zero_banks(7, 1)
            pe.wait_ge(S["steps_ready"], 1)
            with pe.Fori(0, AGG_ITERS) as i:
                blocks = load_blocks(i)
                for s in range(RING):
                    pe.wait_ge(S["hist_s"], RING * i + s + 1)
                    nc.tensor.matmul(PS[0:NP, bass.ds(blocks[s] * 4 + 7 * BANK, 4)], s_bf[:, s, 0:NP],
                                     w4[:, bass.ds(RING * i + s, 1), :].rearrange("p a b -> p (a b)"),
                                     start=False, stop=False, skip_group_check=True).then_inc(S["hist_used"], 1)
            pe.wait_ge(S["tri_in"], 1)
            nc.tensor.matmul(bank(6, NP, NB), tri[:], deg[:], start=True, stop=True).then_inc(S["tri_done"], 1)

            chains = [0]

            def chain(w):
                n = chains[0]
                pe.wait_ge(S["ends_ready"], n + 1)
                nc.tensor.transpose(bank(5, w, P), ends[:, 0:w], ident[:]).then_inc(S["ends_tr"], 1)
                pe.wait_ge(S["carry_in"], n + 1)
                nc.tensor.transpose(bank(6, P, w), carry_row[0:w, 0:P], ident[0:w, 0:w]).then_inc(S["carry_tr"], 1)
                chains[0] += 1

            for w in (1, 2, 1, 1):
                chain(w)
            turn_rows(1)
            pe.wait_ge(S["rows_sb"], ROW_BASE[1] + ROW_UNITS[1])
            agg_pass("l0")
            turn_nodes(1)
            for b in range(NB):
                mm = nc.tensor.matmul(bank(0, NP, D, b * D), HT[:, b, :], wm[:], start=True, stop=True)
            mm.then_inc(S["node_mm"], 1)
            pe.wait_ge(S["tab_ready"], 1)
            zero_banks(0, 7, P)
            with pe.Fori(0, AGG_ITERS) as i:
                for s in range(RING):
                    pe.wait_ge(S["oh_ready"], RING * i + s + 1)
                    for part, rows in ((0, P), (P, D)):
                        for j in range(7):
                            n = min(BANK, N - BANK * j)
                            mm = nc.tensor.matmul(bank(j, rows, n), split(s)[:, part:part + rows],
                                                  onehot(s)[:, j * BANK:j * BANK + n], start=False, stop=False, skip_group_check=True)
                    mm.then_inc(S["ring_used"], 1)
            pe.wait_ge(S["a_sb"], 1)
            for b in range(NB):
                nc.tensor.matmul(bank(0, NP, D, b * D), HT[:, b, :], wu_top[:], start=True, stop=False)
                mm = nc.tensor.matmul(bank(0, NP, D, b * D), big[:, b * NP:(b + 1) * NP], wu_bot2[:], start=False, stop=True)
            mm.then_inc(S["node_mm"], 1)
            for name, j in (("l2a", 2), ("l2b", 3)):
                pe.wait_ge(S["tab_ready"], j)
                agg_pass(name)
            turn_nodes(2)
            pe.wait_ge(S["wasd_ready"], 1)
            for b in range(NB):
                mm = nc.tensor.matmul(bank(7, NP, 2 * H, b * 2 * H), HT[:, b, :], w_asd[:], start=True, stop=True)
            mm.then_inc(S["node_mm"], 1)
            for b in range(NB):
                if b >= 7:
                    pe.wait_ge(S["y_sb"], b - 6)
                nc.tensor.matmul(bank(b % 7, NP, HD), HT[:, b, :], watt[:], start=True, stop=True).then_inc(S["y_bank"], 1)
            for w in (H, 2 * H, H, H):
                chain(w)
            turn_rows(2)
            pe.wait_ge(S["rows_sb"], ROW_BASE[2] + ROW_UNITS[2])
            agg_pass("l3")
            turn_nodes(3)
            for j in range(-(-N // 500)):
                n = min(500, N - 500 * j)
                mm = nc.tensor.matmul(bank(j, P, n), w1_sb[:], free(HT[:, 0, 0:1], [[1, n]], 500 * j), start=True, stop=True)
            mm.then_inc(S["ff1"], 1)
            pe.wait_ge(S["ff1_sb"], 1)
            for b in range(NB):
                mm = nc.tensor.matmul(bank(0, NP, D, b * D), big[:, b * NP:(b + 1) * NP], w2_sb[:], start=True, stop=True)
            mm.then_inc(S["node_mm"], 1)

        @block.vector
        def _(v):
            v_ = nc.vector
            done = [0]

            def go(ins, wait=True):
                done[0] += 1
                ins.then_inc(S["dve"], 1)
                if wait:
                    v.wait_ge(S["dve"], done[0])

            def mark(name):
                v.wait_ge(S["dve"], done[0])
                v.sem_inc(S[name], 1)

            def bc(t, n):
                return free(t, [list(t.ap[1]), [0, n]])

            def vb(j):
                return free(vec[0:NP, j, 0:1], [[0, NB], [1, D]])

            roots = [0]

            def layer_norm(src_t, dst_t):
                go(v_.tensor_reduce(st[:, 0, :], src_t, AX_X, ALU.add))
                go(v_.tensor_scalar(st[:, 0, :], st[:, 0, :], 1.0 / D, None, ALU.mult))
                go(v_.tensor_tensor(T1[:], src_t, bc(st[:, 0, :], D), ALU.subtract))
                go(v_.tensor_tensor(dst_t, T1[:], T1[:], ALU.mult))
                go(v_.tensor_reduce(st[:, 1, :], dst_t, AX_X, ALU.add))
                go(v_.tensor_scalar(st[:, 1, :], st[:, 1, :], 1.0 / D, LN_EPS, ALU.mult, ALU.add))
                inv_root()
                go(v_.tensor_tensor(dst_t, T1[:], bc(st[:, 3, :], D), ALU.mult))

            def inv_root():
                mark("ln_var")
                roots[0] += 1
                v.wait_ge(S["ln_root"], roots[0])
                go(v_.reciprocal(st[:, 3, :], st[:, 2, :]))
                go(v_.tensor_tensor(st[:, 2, :], st[:, 3, :], st[:, 3, :], ALU.mult))
                go(v_.tensor_tensor(st[:, 2, :], st[:, 2, :], st[:, 1, :], ALU.mult))
                go(v_.tensor_scalar(st[:, 2, :], st[:, 2, :], -0.5, 1.5, ALU.mult, ALU.add))
                go(v_.tensor_tensor(st[:, 3, :], st[:, 3, :], st[:, 2, :], ALU.mult))

            v.wait_ge(S["consts"], 1)
            go(v_.tensor_copy(iota_row[:], iota_i[:]))
            go(v_.tensor_copy(iota_bf[:], iota_i[:, 0:NP + 1]))
            go(v_.tensor_copy(tk2[:], kg_i[:]))
            go(v_.memset(idx_pair[:, C:C + RING], 0))
            go(v_.memset(idx_src[:, C:C + RING], 0))
            go(v_.memset(idx_src_k[:, KP:KP + RING], 0))
            go(v_.memset(idx_dst_k[:, KP:KP + RING], 0))
            go(v_.memset(s_ring[:], 0.0))
            v.wait_ge(S["edges_in"], 16 * 11)
            dstf, prevf = junk[:, 0:C], negst
            go(v_.tensor_copy(dstf, dst_i))
            go(v_.tensor_copy(prevf[:], prev_i))
            go(v_.tensor_copy(edge_lin[:, :, 1], src_i))
            go(v_.tensor_copy(edge_lin[:, :, 2], w_lin))
            go(v_.tensor_copy(idx_src[:, 0:C], src_i))
            go(v_.tensor_copy(notst[:], ety_i))
            go(v_.tensor_copy(edge_lin[:, :, 0], dstf))
            go(v_.scalar_tensor_tensor(idx_pair[:, 0:C], edge_lin[:, :, 1], float(RELS), notst[:], ALU.mult, ALU.add))
            mark("edges_ready")
            go(v_.tensor_tensor(notst[:], dstf, prevf[:], ALU.is_equal))
            go(v_.tensor_scalar(negst[:], notst[:], 1.0, BIG, ALU.subtract, ALU.mult))
            go(v_.tensor_reduce(cnt[:, 0:1], notst[:], AX_X, ALU.min))
            go(v_.tensor_scalar(chain_in[:], ones[:, 0:2 * H], cnt[:, 0:1], None, ALU.mult))
            go(v_.memset(cnt[:, 0:1], 0.0))
            go(v_.memset(cnt[:, NB:NB + 1], float(E) / P))
            for b in range(1, NB):
                go(v_.tensor_scalar(bk[:, 0:C], dstf, float(b * NP), None, ALU.is_lt, ALU.add, accum_out=cnt[:, b:b + 1]))
            mark("cnt_ready")
            v.wait_ge(S["chain_tr"], 1)
            go(v_.tensor_copy(cf_sum[:], bank(4, 2 * H, P)))
            go(v_.tensor_copy(R[:], bank(3, P, NB + 1)))
            go(v_.tensor_scalar(cf_max[:], cf_sum[:], 1.0, BIG, ALU.subtract, ALU.mult))
            first, last, nst, off, delta, dd, tot = (small[:, j, 0:NB] for j in range(7))
            go(v_.tensor_scalar(last, R[:, 1:NB + 1], 1.0, None, ALU.subtract))
            go(v_.tensor_tensor(last, last, R[:, 0:NB], ALU.max))
            go(v_.tensor_copy(small_i[:, 0, 0:NB], R[:, 0:NB]))
            go(v_.tensor_copy(small_i[:, 1, 0:NB], last))
            go(v_.tensor_scalar(small_i[:, :, 0:NB], small_i[:, :, 0:NB], 7, None, ALU.logical_shift_right))
            go(v_.tensor_copy(first, small_i[:, 0, 0:NB]))
            go(v_.tensor_copy(last, small_i[:, 1, 0:NB]))
            go(v_.tensor_tensor(nst, last, first, ALU.subtract))
            go(v_.tensor_scalar(nst, nst, 1.0, None, ALU.add))
            go(v_.tensor_tensor_scan(tot, ones[:, 0:NB], nst, 0.0, ALU.mult, ALU.add))
            go(v_.tensor_tensor(off, tot, nst, ALU.subtract))
            go(v_.tensor_tensor(delta, first, off, ALU.subtract))
            go(v_.tensor_tensor(dd[:, 1:NB], delta[:, 1:NB], delta[:, 0:NB - 1], ALU.subtract))
            go(v_.tensor_copy(tk[:], tk2[:]))
            for b in range(1, NB):
                go(v_.tensor_scalar(small[:, 7, 0:KG], tk2[:], off[:, b:b + 1], dd[:, b:b + 1], ALU.is_ge, ALU.mult))
                go(v_.tensor_tensor(tk[:], tk[:], small[:, 7, 0:KG], ALU.add))
            go(v_.tensor_scalar(small[:, 7, 0:KG], tk2[:], tot[:, NB - 1:NB], float(PAD_TILE), ALU.is_ge, ALU.mult))
            go(v_.tensor_tensor(tk[:], tk[:], small[:, 7, 0:KG], ALU.add))
            go(v_.tensor_scalar(tk_i[:], tk[:], float(PAD_TILE), None, ALU.min))
            mark("tk_ready")
            go(v_.memset(bk[:], 0.0))
            for b in range(1, NB):
                go(v_.scalar_tensor_tensor(bk[:], iota_row[:], off[:, b:b + 1], bk[:], ALU.is_ge, ALU.add))
            go(v_.tensor_copy(bk_i[:], bk[0:1, :]))
            v.wait_ge(S["wtr"], 1)
            go(v_.tensor_copy(w1T[:], bank(0, D, 3 * D)))
            go(v_.tensor_copy(embT[:], bank(1, D, RELS)))
            mark("wtr_sb")
            v.wait_ge(S["vproj"], 1)
            go(v_.tensor_copy(vv[:], bank(2, D, 3)))
            go(v_.tensor_copy(rhs0[:, D:D + 2], vv[:, 0:2]))
            go(v_.tensor_scalar(vr_b[:], ones[0:D, :], vv[:, 2:3], None, ALU.mult))
            v.wait_ge(S["x_in"], 16)
            v.wait_ge(S["vecs_in"], 16 * 8)
            v.wait_ge(S["weights_in"], 16 * 12)
            layer_norm(X[:], Hn[:])
            go(v_.tensor_scalar(Hn[:], Hn[:], 0.0, None, ALU.max))
            mark("h_ready")
            v.wait_ge(S["node_mm"], 1)
            for j in range(-(-NB // PERB)):
                n = min(PERB, NB - PERB * j)
                ps = bank(j, NP, PERB * P).rearrange("p (n c) -> p n c", c=P)
                go(v_.tensor_copy(T2[:, PERB * j:PERB * j + n, :], ps[:, 0:n, 0:D]))
                go(v_.tensor_copy(nfl[:, 0, PERB * j:PERB * j + n], ps[:, 0:n, D]))
                go(v_.tensor_copy(nfl[:, 1, PERB * j:PERB * j + n], ps[:, 0:n, D + 1]))
            v.wait_ge(S["edges_out"], 16)
            for b in range(NB):
                go(v_.tensor_scalar(big[0:NP, b * RELS:(b + 1) * RELS], bank(7, NP, RELS), nfl[:, 0, b:b + 1], None, ALU.add), False)
            mark("pair_ready")
            v.wait_ge(S["rows_sb"], ROW_UNITS[0])
            v.wait_ge(S["pair_out"], 16)
            t_f, s_f, w_f = (steps3[:, j * KP:(j + 1) * KP] for j in range(3))
            v1 = junk[:, 0:KP]
            go(v_.scalar_tensor_tensor(dstl[:], bk[:], -float(NP), t_f, ALU.mult, ALU.add))
            go(v_.tensor_scalar(v1, dstl[:], 0.0, None, ALU.is_ge))
            go(v_.scalar_tensor_tensor(v1, dstl[:], float(NP), v1, ALU.is_lt, ALU.mult))
            go(v_.scalar_tensor_tensor(srcm[:], s_f, 1.0, v1, ALU.add, ALU.mult))
            go(v_.tensor_scalar(srcm[:], srcm[:], 1.0, None, ALU.subtract))
            go(v_.tensor_copy(idx_src_k[:, 0:KP], s_f))
            go(v_.tensor_scalar(idx_dst_k[:, 0:KP], t_f, float(N - 1), None, ALU.min))
            go(v_.tensor_copy(wk[:], w_f))
            go(v_.memset(w4[:, :, 0], 1.0))
            go(v_.tensor_copy(w4[:, :, 1], w_f))
            go(v_.tensor_tensor(v1, w_f, w4[:, :, 1], ALU.subtract))
            go(v_.tensor_copy(w4[:, :, 2], v1))
            go(v_.tensor_tensor(v1, v1, w4[:, :, 2], ALU.subtract))
            go(v_.tensor_copy(w4[:, :, 3], v1))
            mark("steps_ready")
            with v.Fori(0, AGG_ITERS) as i:
                for s in range(RING):
                    v.wait_ge(S["hist_used"], RING * i + s + 1)
                    v_.tensor_scalar(s_bf[:, s, 0:NP], iota_bf[:, 0:NP], dstl[:, bass.ds(RING * i + s, 1)], None,
                                     ALU.is_equal).then_inc(S["hist_s"], 1)
            v.wait_ge(S["hist_used"], K + RING)
            hist = bank(7, NP, 4 * NB).rearrange("p (b k) -> p b k", k=4)
            go(v_.tensor_copy(deg[:], hist[:, :, 0]))
            go(v_.tensor_reduce(norm[:], hist[:, :, 1:4], AX_X, ALU.add))
            mark("tri_in")
            v.wait_ge(S["tri_done"], 1)
            start, has, tmp = nfl[:, 2, :], nfl[:, 3, :], st[:, 0, :]
            go(v_.tensor_tensor(start, bank(6, NP, NB), R[0:NP, 0:NB], ALU.add))
            go(v_.tensor_scalar(has, deg[:], 0.0, None, ALU.is_equal))
            go(v_.scalar_tensor_tensor(tmp, has, OUT_OF_RANGE, start, ALU.mult, ALU.add))
            go(v_.tensor_copy(start_i[:], tmp))
            go(v_.tensor_tensor(tmp, tmp, deg[:], ALU.add))
            go(v_.tensor_scalar(last_i[:], tmp, 1.0, None, ALU.subtract))
            mark("idx_ready")

            chains = [0]

            def scan_all(buf, out_buf, w, flags, cf, op0, neutral):
                same = buf is out_buf
                for j in range(w):
                    if same:
                        go(v_.tensor_tensor_scan(junk[:, 0:C], flags[:], col(buf, j, w), neutral, op0[0], op0[1]))
                        go(v_.tensor_copy(ends[:, j:j + 1], junk[:, C - 1:C]))
                    else:
                        go(v_.tensor_tensor_scan(col(out_buf, j, w), flags[:], col(buf, j, w), neutral, op0[0], op0[1]), False)
                if not same:
                    v.wait_ge(S["dve"], done[0])
                    go(v_.tensor_copy(ends[:, 0:w], free(out_buf[:, 0:1], [[1, w]], (C - 1) * w)))
                n = chains[0]
                mark("ends_ready")
                v.wait_ge(S["ends_tr"], n + 1)
                go(v_.memset(carry_row[0:w, 0:1], neutral))
                go(v_.tensor_tensor_scan(carry_row[0:w, 1:P + 1], cf[0:w, :], bank(5, w, P), neutral, op0[0], op0[1]))
                mark("carry_in")
                v.wait_ge(S["carry_tr"], n + 1)
                go(v_.tensor_copy(carry[:, 0:w], bank(6, P, w)))
                for j in range(w):
                    go(v_.tensor_tensor_scan(col(out_buf, j, w), flags[:], col(buf, j, w), carry[:, j:j + 1], op0[0], op0[1]), False)
                chains[0] += 1

            MAXOP, SUMOP = (ALU.add, ALU.max), (ALU.mult, ALU.add)

            def softmax(turn, nh, slope):
                w = nh * C
                q = qa[:, 0:w]
                q3 = q.rearrange("p (c k) -> p c k", k=nh)
                fa = big[:, 0:2 * w].rearrange("p (c k) -> p c k", k=2 * nh)
                fb, sm = big[:, w:2 * w], big[:, 0:w]
                mx, den, fill, me = packed(nmx, nh), packed(nden, nh), packed(nfill, 2 * nh), packed(nself, nh)
                go(v_.memset(nmx[:], -BIG))
                go(v_.memset(nden[:], 0.0))
                mark("nmx_ready")
                name = "pair" if turn == 0 else "as"
                v.wait_ge(S["ring_used"], RING * (BASE[name] + ITERS[name] + 1))
                scan_all(q, sm, nh, negst, cf_max, MAXOP, -BIG)
                mark("scan_ready")
                v.wait_ge(S["nodes_in"], 16 * NB * (2 * turn + 1))
                if turn == 0:
                    go(v_.tensor_copy(fill[:, :, 0], nfl[:, 1, :]))
                else:
                    a_s, a_d = asd[:, :, 0:H], asd[:, :, H:2 * H]
                    go(v_.tensor_copy(fill[:, :, 0:nh], a_d))
                    go(v_.tensor_tensor(mx, mx, a_s, ALU.max))
                    go(v_.tensor_tensor(me, a_s, a_d, ALU.add))
                    go(v_.scalar_tensor_tensor(me, me, slope, me, ALU.mult, ALU.max))
                go(v_.tensor_tensor(mx, mx, fill[:, :, 0:nh], ALU.add))
                go(v_.scalar_tensor_tensor(fill[:, :, nh:2 * nh], mx, slope, mx, ALU.mult, ALU.max))
                if turn == 1:
                    go(v_.tensor_tensor(me, me, fill[:, :, nh:2 * nh], ALU.subtract))
                mark("fill_ready")
                v.wait_ge(S["fill_in"], 16 * (2 * turn + 1))
                fbuf = big[:, 0:2 * w]
                scan_all(fbuf, fbuf, 2 * nh, notst, cf_sum, SUMOP, 0.0)
                v.wait_ge(S["dve"], done[0])
                go(v_.tensor_tensor(q3, q3, fa[:, :, 0:nh], ALU.add))
                go(v_.scalar_tensor_tensor(q, q, slope, q, ALU.mult, ALU.max))
                go(v_.tensor_tensor(q3, q3, fa[:, :, nh:2 * nh], ALU.subtract))
                go(v_.tensor_scalar(q, q, 0.0, None, ALU.min))
                mark("exp_in")
                v.wait_ge(S["exp_done"], turn + 1)
                scan_all(q, sm, nh, notst, cf_sum, SUMOP, 0.0)
                mark("scan_ready")
                v.wait_ge(S["nodes_in"], 16 * NB * (2 * turn + 2))
                pack_b = packed(nfill, nh)
                if turn == 0:
                    go(v_.tensor_tensor(den, den, bc(nfl[:, 3, :], 1), ALU.add))
                    go(v_.reciprocal(pack_b, den))
                else:
                    go(v_.tensor_tensor(den, den, me, ALU.add))
                    go(v_.tensor_scalar(den, den, SM_EPS, float(nh), ALU.add, ALU.mult))
                    go(v_.reciprocal(pack_b, den))
                    go(v_.tensor_tensor(me, me, pack_b, ALU.mult))
                mark("fill_ready")
                v.wait_ge(S["fill_in"], 16 * (2 * turn + 2))
                scan_all(fb, fb, nh, notst, cf_sum, SUMOP, 0.0)
                v.wait_ge(S["dve"], done[0])
                go(v_.tensor_tensor(q, q, fb, ALU.mult))
                mark("alpha_ready")

            def one_hots(name, val):
                base = BASE[name]
                with v.Fori(0, AGG_ITERS) as i:
                    for s in range(RING):
                        v.wait_ge(S["ring_used"], RING * i + (RING * base + s + 1))
                        v_.tensor_scalar(s_ring[:, s, 0:NP], iota_row[:, 0:NP], dstl[:, bass.ds(RING * i + s, 1)],
                                         val[:, bass.ds(RING * i + s, 1)], ALU.is_equal, ALU.mult).then_inc(S["s_ready"], 1)
                v.wait_ge(S["ring_used"], RING * (base + AGG_ITERS + 1))

            softmax(0, 1, 0.01)
            v.wait_ge(S["rows_sb"], ROW_BASE[1] + ROW_UNITS[1])
            one_hots("l0", alpha0)
            go(v_.tensor_tensor(T1[:], Hn[:], bc(nfl[:, 3, :], D), ALU.mult))
            go(v_.tensor_tensor(T1[:], T1[:], T2[:], ALU.add))
            go(v_.tensor_tensor(T1[:], T1[:], agg_psum(), ALU.add))
            go(v_.scalar_tensor_tensor(X[:], T1[:], 0.0, X[:], ALU.max, ALU.add))
            layer_norm(X[:], Hn[:])
            go(v_.tensor_scalar(Hn[:], Hn[:], 0.0, None, ALU.max))
            mark("h_ready")
            v.wait_ge(S["node_mm"], 2)
            go(v_.tensor_tensor(T1[:], agg_psum(), vb(BM), ALU.add))
            mark("tab_ready")
            base = BASE["l1"]
            with v.Fori(0, AGG_ITERS) as i:
                for h in range(2):
                    lo, hi = HALF * h, HALF * h + HALF
                    for s in range(lo, hi):
                        v.wait_ge(slot[s], 16 * i + 16 * (base + 1))
                    v.wait_ge(S["ring_used"], RING * i + (RING * base + hi))
                    F = ring[:, lo:hi, :]
                    v_.tensor_copy(parts(lo, hi, 0), F).then_inc(S["split_dve"], 1)
                    v.wait_ge(S["split_dve"], 8 * i + (4 * h + 1))
                    v_.tensor_tensor(fres[:, lo:hi, :], F, parts(lo, hi, 0), ALU.subtract).then_inc(S["split_dve"], 1)
                    v.wait_ge(S["split_dve"], 8 * i + (4 * h + 2))
                    v_.tensor_copy(parts(lo, hi, 1), fres[:, lo:hi, :]).then_inc(S["split_dve"], 1)
                    v.wait_ge(S["split_dve"], 8 * i + (4 * h + 3))
                    v_.tensor_tensor(parts(lo, hi, 2), fres[:, lo:hi, :], parts(lo, hi, 1), ALU.subtract).then_inc(S["split_dve"], 1)
                    v.wait_ge(S["split_dve"], 8 * i + (4 * h + 4))
                    for s in range(lo, hi):
                        v.wait_ge(S["ring_used"], RING * i + (RING * base + s + 1 + RING - OHS))
                        v_.tensor_scalar(onehot(s), iota_n, srcm[:, bass.ds(RING * i + s, 1)], None,
                                         ALU.is_equal).then_inc(S["oh_ready"], 1)
            v.wait_ge(S["ring_used"], RING * (base + AGG_ITERS + 1))
            for j in range(7):
                n = min(BANK, N - BANK * j)
                go(v_.tensor_copy(big[:, j * BANK:j * BANK + n], bank(j, P, n)))
            mark("a_sb")
            v.wait_ge(S["node_mm"], 3)
            go(v_.tensor_tensor(T1[:], agg_psum(), vb(BU), ALU.add))
            go(v_.scalar_tensor_tensor(X[:], T1[:], 0.0, X[:], ALU.max, ALU.add))
            layer_norm(X[:], Hn[:])
            go(v_.tensor_scalar(Hn[:], Hn[:], 0.0, None, ALU.max))
            go(v_.tensor_scalar(st[:, 1, :], norm[:], 1.0, None, ALU.max))
            inv_root()
            go(v_.tensor_copy(norm[:], st[:, 3, :]))
            go(v_.tensor_tensor(T1[:], Hn[:], bc(norm[:], D), ALU.mult))
            mark("tab_ready")
            one_hots("l2a", wk)
            go(v_.tensor_tensor(T1[:], agg_psum(), bc(norm[:], D), ALU.mult))
            go(v_.tensor_tensor(T2[:], Hn[:], T1[:], ALU.add))
            v.wait_ge(S["tab_out"], 16 * 3)
            go(v_.tensor_tensor(T1[:], T1[:], bc(norm[:], D), ALU.mult))
            mark("tab_ready")
            one_hots("l2b", wk)
            go(v_.tensor_tensor(T1[:], agg_psum(), bc(norm[:], D), ALU.mult))
            go(v_.tensor_tensor(T2[:], T2[:], T1[:], ALU.add))
            go(v_.scalar_tensor_tensor(X[:], T2[:], 1.0 / 3.0, X[:], ALU.mult, ALU.add))
            v.wait_ge(S["watt_in"], 32)
            for j in range(2):
                go(v_.tensor_tensor(big[0:D, 0:HD], watt[:], att_b[:, j, :], ALU.mult))
                go(v_.tensor_reduce(w_asd[:, j * H:(j + 1) * H], big[0:D, 0:HD].rearrange("p (h c) -> p h c", h=H), AX_X, ALU.add))
            mark("wasd_ready")
            layer_norm(X[:], Hn[:])
            go(v_.tensor_scalar(Hn[:], Hn[:], 0.0, None, ALU.max))
            mark("h_ready")
            v.wait_ge(S["node_mm"], 4)
            go(v_.tensor_copy(asd[:], bank(7, NP, 2 * H * NB).rearrange("p (b k) -> p b k", b=NB)))
            mark("asd_sb")
            v.wait_ge(S["y_out"], 32)
            softmax(1, H, 0.2)
            v.wait_ge(S["rows_sb"], ROW_BASE[2] + ROW_UNITS[2])
            base = BASE["l3"]
            a3 = qa[:, :].rearrange("p (h k) -> p h k", h=H)
            with v.Fori(0, AGG_ITERS) as i:
                for s in range(RING):
                    v.wait_ge(slot[s], 16 * i + 16 * (base + 1))
                    v.wait_ge(S["ring_used"], RING * i + (RING * base + s + 1 + RING - PR))
                    al = a3[:, :, bass.ds(RING * i + s, 1)]
                    v_.tensor_tensor(prod[:, s % PR, :].rearrange("p (h f) -> p h f", h=H),
                                     yring[:, s % (RING // 2), :].rearrange("p (h f) -> p h f", h=H),
                                     al.to_broadcast([P, H, D]), ALU.mult).then_inc(S["prod_done"], 1)
                    v_.tensor_scalar(s_ring[:, s, 0:NP], iota_row[:, 0:NP], dstl[:, bass.ds(RING * i + s, 1)],
                                     None, ALU.is_equal)
                    v.wait_ge(S["prod_done"], RING * i + s + 1)
                    v_.tensor_tensor(prod[:, s % PR, 0:HD // 2], prod[:, s % PR, 0:HD // 2], prod[:, s % PR, HD // 2:HD],
                                     ALU.add).then_inc(S["s_ready"], 1)
            v.wait_ge(S["ring_used"], RING * (base + AGG_ITERS + 1))
            v.wait_ge(S["y_back"], 16)
            y4 = big[0:NP, :].rearrange("p (k f) -> p k f", f=D)
            go(v_.tensor_tensor(y4, y4, free(nself[:, 0, 0:1], [[1, NB * H], [0, D]]), ALU.mult))
            go(v_.tensor_reduce(T2[:], big[0:NP, :].rearrange("p (b h f) -> p b f h", b=NB, h=H), AX_X, ALU.add))
            go(v_.tensor_tensor(T2[:], T2[:], agg_psum(), ALU.add))
            go(v_.tensor_tensor(T2[:], T2[:], vb(BA), ALU.add))
            go(v_.tensor_tensor(T2[:], T2[:], Hn[:], ALU.add))
            layer_norm(T2[:], Hn[:])
            go(v_.tensor_tensor(Hn[:], Hn[:], vb(G1), ALU.mult))
            go(v_.tensor_tensor(Hn[:], Hn[:], vb(E1), ALU.add))
            mark("h_ready")
            v.wait_ge(S["node_mm"], 5)
            go(v_.tensor_tensor(T2[:], agg_psum(), vb(B2), ALU.add))
            go(v_.tensor_tensor(T2[:], T2[:], Hn[:], ALU.add))
            layer_norm(T2[:], Hn[:])
            go(v_.tensor_tensor(Hn[:], Hn[:], vb(G2), ALU.mult))
            go(v_.tensor_tensor(Hn[:], Hn[:], vb(E2), ALU.add))
            go(v_.tensor_tensor(X[:], X[:], Hn[:], ALU.add))
            mark("x_done")


_INS = ['x', 'src', 'dst', 'edge_type_200', 'edge_weight', 'L0_gnn_emb_rel', 'L0_gnn_loop_weight', 'L0_gnn_attn_w1',
        'L0_gnn_attn_w2', 'L1_gnn_W_msg', 'L1_gnn_b_msg', 'L1_gnn_W_upd', 'L1_gnn_b_upd', 'L3_gnn_W_att',
        'L3_gnn_att_src', 'L3_gnn_att_dst', 'L3_gnn_bias_att', 'L3_gnn_W1', 'L3_gnn_b1', 'L3_gnn_W2', 'L3_gnn_b2',
        'L3_gnn_ln1_g', 'L3_gnn_ln1_b', 'L3_gnn_ln2_g', 'L3_gnn_ln2_b']


def kernel(**inputs):
    import numpy as _np
    import concourse.bacc as _bacc
    from concourse import mybir as _mybir
    from concourse.bass_utils import run_bass_kernel_spmd as _run

    nc = _bacc.Bacc("TRN2", target_bir_lowering=False, num_devices=1)
    arrays, args = {}, []
    for name in _INS:
        a = _np.ascontiguousarray(inputs[name])
        arrays[f"in_{name}_dram"] = a
        args.append(nc.dram_tensor(f"in_{name}_dram", a.shape, _mybir.dt.from_np(a.dtype), kind="ExternalInput").ap())
    args.append(nc.dram_tensor("out_0_dram", inputs["x"].shape, _mybir.dt.float32, kind="ExternalOutput").ap())
    gnn_four_layers(nc, *args)
    r = _run(nc, [arrays], core_ids=[0])
    return r.results[0]["out_0_dram"]
```

```python
from contextlib import ExitStack

import concourse.bass as bass
from concourse import mybir

ALU = mybir.AluOpType
ACT = mybir.ActivationFunctionType
AX_X = mybir.AxisListType.X
F32 = mybir.dt.float32
BF16 = mybir.dt.bfloat16
I32 = mybir.dt.int32

P = 128
RING = 16
HALF = RING // 2
BIG = 1.0e38
LN_EPS = 1e-5
SM_EPS = 1e-16


def free(ap, dims, offset=0):
    return bass.AP(ap.tensor, ap.offset + offset, [list(ap.ap[0]), *[list(d) for d in dims]])


def rows_on_all(dram, parts):
    n = 1
    for s in dram.shape:
        n *= s
    return bass.AP(dram.tensor, dram.offset, [[0, parts], [1, n]])




def gnn_four_layers(
    nc, x, src, dst, etype, weight, emb_rel, loop_weight, attn_w1, attn_w2, W_msg, b_msg, W_upd, b_upd,
    W_att, att_src, att_dst, bias_att, W1, b1, W2, b2, ln1_g, ln1_b, ln2_g, ln2_b, out,
):
    N, D = x.shape
    E = src.shape[0]
    RELS = emb_rel.shape[0]
    H = att_src.shape[0]
    NP = 125
    NB = N // NP
    assert NB * NP == N and D == 64
    C = -(-E // (P * RING)) * RING
    EP = P * C
    FULL = E // C
    REST = E - FULL * C
    assert FULL == P - 1 and C * P * RING >= E
    TILES = -(-E // P)
    K = -(-(TILES + NB - 1) // RING) * RING
    KG = -(-K // P)
    KP = KG * P
    LIN_ITERS = C // RING
    AGG_ITERS = K // RING
    WN = 5
    WB = NP // WN
    NW = N // WN
    CUTS = (0, (WB + 1) // 2, WB)
    UD = 8
    QB = UD // 2
    W = NP + 1
    assert WN * NB == NP and WB * WN == NP
    KD = TILES + NW - 1 + 2 * NB * (UD - 1)
    DG = -(-KD // P)
    DP = DG * P
    assert KD + UD <= DP
    PAD_TILE = C - 1
    assert TILES <= PAD_TILE
    OUT_OF_RANGE = 2.0 * EP
    HD = H * D
    BANK = 512
    PERB = 4

    ctx = ExitStack()
    with ctx:
        def sb(name, shape, dt=F32):
            return ctx.enter_context(nc.sbuf_tensor(name, shape, dt))

        def sem(name):
            return ctx.enter_context(nc.semaphore(name))

        def dram(name, shape, dt=F32):
            return nc.dram_tensor(name, shape, dt).ap()

        d_edges = dram("d_edges", (EP, 3))
        d_dense = dram("d_dense", (EP, 3))
        d_pos = dram("d_pos", (DG, P), I32)
        d_cnt = dram("d_cnt", (NB, NP, N))
        d_wgt = dram("d_wgt", (NB, NP, N))
        d_pair = dram("d_pair", (N * RELS, 1))
        d_h0 = dram("d_h0", (N, D))
        d_y = dram("d_y", (N, HD))
        d_max0, d_sum0 = dram("d_max0", (EP, 1)), dram("d_sum0", (EP, 1))
        d_max3, d_sum3 = dram("d_max3", (EP, H)), dram("d_sum3", (EP, H))
        d_fa0, d_fb0 = dram("d_fa0", (EP, 2)), dram("d_fb0", (EP, 1))
        d_fa3, d_fb3 = dram("d_fa3", (EP, 2 * H)), dram("d_fb3", (EP, H))
        d_al0, d_al3 = dram("d_al0", (EP, 1)), dram("d_al3", (EP, H))

        PS = ctx.enter_context(nc.psum_tensor("PS", [P, 8 * BANK], F32))

        ident = sb("ident", [P, P])
        ones = sb("ones", [P, P])
        tri = sb("tri", [NP, NP])
        iota_row = sb("iota_row", [P, KP])
        iota_bf = sb("iota_bf", [P, NP + 1], BF16)
        kg_i = sb("kg_i", [P, KG], I32)
        zero_bf = sb("zero_bf", [P, BANK], BF16)

        w1t_in = sb("w1t_in", [D, 3, D])
        w2_col = sb("w2_col", [D, 1])
        emb = sb("emb", [RELS // 2, 2, D])
        w1T = sb("w1T", [D, 3 * D])
        embT = sb("embT", [D, RELS])
        vv = sb("vv", [D, 3])
        vr_b = sb("vr_b", [D, P])
        rhs0 = sb("rhs0", [D, D + 2])
        wm = sb("wm", [D, D])
        wu_top = sb("wu_top", [D, D])
        wu_bot = sb("wu_bot", [D, D])
        wmT = sb("wmT", [D, D])
        wmu = sb("wmu", [D, D])
        bm_col = sb("bm_col", [D, 1])
        bm_b = sb("bm_b", [D, P])
        watt = sb("watt", [D, HD])
        w_asd = sb("w_asd", [D, 2 * H])
        w1_sb = sb("w1_sb", [D, 2 * D])
        b1_col = sb("b1_col", [2 * D, 1])
        w2_sb = sb("w2_sb", [2 * D, D])
        vec = sb("vec", [P, 8, D])
        BM, BU, BA, B2, G1, E1, G2, E2 = range(8)

        big = sb("big", [P, NB * HD])
        ints = big[:, 0:3 * C].bitcast(I32)
        dst_i, prev_i, src_i = (ints[:, j * C:(j + 1) * C] for j in range(3))
        ety_i = big[:, 3 * C:4 * C].bitcast(I32)
        w_lin = big[:, 4 * C:5 * C]
        edge_lin = free(big[:, 5 * C:5 * C + 1], [[3, C], [1, 3]])
        junk = sb("junk", [P, max(C, KP)])
        iota_i = junk[:, 0:KP].bitcast(I32)

        notst = sb("notst", [P, C])
        negst = sb("negst", [P, C])
        cf_sum = sb("cf_sum", [2 * H, P])
        cf_max = sb("cf_max", [2 * H, P])
        chain_in = sb("chain_in", [P, 2 * H])
        idx_pair = sb("idx_pair", [P, C + RING], I32)
        lo_b = sb("lo_b", [P, C], BF16)
        hi_b = sb("hi_b", [P, C], BF16)
        cnt = sb("cnt", [P, NB + 1])
        R = sb("R", [P, NB + 1])
        small = sb("small", [P, 8, NB + 1])
        small_i = sb("small_i", [P, 2, NB + 1], I32)
        tk = sb("tk", [P, KG])
        tk2 = sb("tk2", [P, KG])
        tk_i = sb("tk_i", [P, KG], I32)
        bk = sb("bk", [P, KP])
        bk_i = sb("bk_i", [1, KP], I32)

        dstl = sb("dstl", [P, KP])
        idx_src_k = sb("idx_src_k", [P, KP + RING], I32)
        w4 = sb("w4", [P, KP, 4], BF16)
        alpha0 = bk
        qa = sb("qa", [P, KP * H])
        zrow = qa[:, 0:C]
        idx_ring = sb("idx_ring", [P, RING], I32)
        ring = sb("ring", [P, RING, D])
        yring = big[:, 0:RING * HD].rearrange("p (s m) -> p s m", m=HD)
        s_ring = sb("s_ring", [P, RING, NP + 1])
        s_bf = s_ring.rearrange("p s m -> p (s m)")[:, 0:RING * W // 2].bitcast(BF16)
        iota_h = big[:, 0:W * HALF // 2].bitcast(BF16)
        dst_b = big[:, W * HALF // 2:W * HALF // 2 + KP // 2].bitcast(BF16)
        MB = 4
        PR = 2 * MB
        prod = big[:, RING * HD:(RING + PR) * HD].rearrange("p (s m) -> p s m", m=HD)

        dense_lin = free(big[:, 8 * C:8 * C + 1], [[3, C], [1, 3]])
        drow = big[:, big.shape[1] - DG * P * 3:]
        dcols = qa[:, C:C + 3 * DP]
        d_lo, d_c, d_w = (dcols[:, j * DP:(j + 1) * DP] for j in range(3))
        tabs = big[:, 2 * N:2 * N + (5 * DP + 1) // 2].bitcast(BF16)
        assert 2 * N + (5 * DP + 1) // 2 <= big.shape[1] and DP % 2 == 0
        hots = qa[:, C:C + 5 * UD * W // 2].bitcast(BF16)
        iota_q = qa[:, C + 5 * UD * W // 2:C + 5 * UD * W // 2 + QB * W // 2].bitcast(BF16)
        assert C + 5 * UD * W // 2 + QB * W // 2 <= qa.shape[1]

        def hot(h, first, n):
            return free(hots[:, 0:1], [[W * QB, n], [QB, W], [1, QB]], (h * 5 + first) * W * QB)

        def hot_step(h, j, first, n):
            return free(hots[:, 0:1], [[W * QB, n], [QB, W]], (h * 5 + first) * W * QB + j)
        kg5_i = sb("kg5_i", [P, DG], I32)
        k5 = sb("k5", [P, 6, DG])
        tk5_i = sb("tk5_i", [P, DG], I32)
        tk2i = sb("tk2i", [P, DG], I32)
        pos_c = sb("pos_c", [DG, P], I32)
        pos_i = sb("pos_i", [1, DP], I32)
        cut_i = sb("cut_i", [1, 2 * NB + 1], I32)
        sel5 = sb("sel5", [NP, WB])
        TW = NW + 15
        rank_in = big[0:NP, 9 * TW:9 * TW + NW]
        assert 10 * TW <= big.shape[1] - 3 * DG * P + 1600
        idx_f = bk

        def tw(j, i32=False):
            t = big[:, j * TW:j * TW + NW + 1]
            return t.bitcast(I32) if i32 else t

        LW = NP + 3
        blk_c, blk_w = big[0:NP, 0:N], big[0:NP, N:2 * N]
        blk_in = big[0:NP, 0:3 * N].rearrange("p (s m) -> p s m", s=3)
        blk_t = big[0:NP, 3 * N:3 * N + NB * LW].rearrange("p (g m) -> p g m", m=LW)
        T_ROW = 3 * N + NB * LW
        t_row = big[0:NP, T_ROW:T_ROW + 3 * D].rearrange("p (s m) -> p s m", s=3)
        BB = 3
        assert (NB - 1) % BB == 0 and T_ROW + 3 * D <= big.shape[1]

        def loads_before(turn, j):
            return turn * ((NB - 1) // BB + (j == 0))

        CB, HN = 4, H * NB
        assert CB == QB and C % (2 * CB) == 0
        LOOK_GROUPS = C // CB
        hot_hi = big[:, 0:C * NB // 2].bitcast(BF16)
        at = C * NB // 2
        src_parts = big[0:NP, at:at + 3 * HN // 2].bitcast(BF16)
        src_left = big[0:NP, at + 3 * HN // 2:at + 3 * HN // 2 + HN]
        at += 3 * HN // 2 + HN
        picked = big[:, at:at + CB * HN]
        at += CB * HN
        look_hot = big[:, at:at + CB * W].bitcast(BF16)
        at += CB * W
        iota_look = big[:, at:at + CB * W // 2].bitcast(BF16)
        at += CB * W // 2
        ident_bf = big[:, at:at + P // 2].bitcast(BF16)
        assert at + P // 2 <= big.shape[1]
        look_t = ring[:, 0:CB * P // D, :].rearrange("p a b -> p (a b)").bitcast(BF16).rearrange("p (s m) -> p s m", s=2)

        att_b = big[0:D, HD:3 * HD].rearrange("p (j m) -> p j m", j=2)

        X = sb("X", [NP, NB, D])
        Hn = sb("Hn", [NP, NB, D])
        T1 = sb("T1", [NP, NB, D])
        T2 = sb("T2", [NP, NB, D])
        HT = sb("HT", [D, NB, NP])
        st = sb("st", [NP, 4, NB])
        deg = sb("deg", [NP, NB])
        norm = sb("norm", [NP, NB])
        start_i = sb("start_i", [NP, NB], I32)
        last_i = sb("last_i", [NP, NB], I32)
        nfl = sb("nfl", [NP, 4, NB])
        asd = sb("asd", [NP, NB, 2 * H])
        nmx = sb("nmx", [NP, NB, H])
        nfill = sb("nfill", [NP, NB, 2 * H])
        nself = sb("nself", [NP, NB, H])
        nden = sb("nden", [NP, NB, H])
        ends = sb("ends", [P, 2 * H])
        carry_row = sb("carry_row", [2 * H, P + 1])
        carry = sb("carry", [P, 2 * H])

        names = """consts preinc pads edges_in weights_in x_in vecs_in zero_ready fills_zero wtr wtr_sb vproj
            h_ready ht_psum ht_sb node_mm asd_sb pair_ready pair_out edges_ready edges_out cnt_ready
            tk_ready rows_in rows_tr rows_sb steps_ready hist_s hist_used tri_in tri_done idx_ready staged
            ring_used s_ready prod_done ends_ready ends_tr carry_in carry_tr chain_tr scan_ready scan_out
            nodes_in fill_ready fill_out fill_in alpha_ready alpha_out tab_ready tab_out dve halves_begun
            ln_var ln_root x_done out_done y_bank y_sb y_out y_back watt_in wasd_ready ff1 ff1_sb exp_in
            exp_done nmx_ready dense_out rank_in r5_tr k5_ready drows_in drows_tr drows_sb kpos_tr kpos_sb
            pos_out pos_in dense_ready hot_ready one_ready one_used share0_sb share1_sb blk_out q_out0
            q_out1 stage_in0 stage_in1 blk_in0 blk_in1 blk_in2 neigh_sb neigh_tr look_hot look_tr look_t
            look_mm look_used look_sum blk_used ct_tr ct_sb ct_used""".split()
        S = {n: sem(n) for n in names}
        slot = [sem(f"slot{i}") for i in range(RING)]

        PASSES = [("pair", LIN_ITERS), ("l0", AGG_ITERS), ("l3", AGG_ITERS)]
        ITERS = dict(PASSES)
        LIN_TURN = {"pair": 0}
        USED_BASE = {"l0": 0, "l3": K}
        STAGED_BASE = {"l0": 0, "l3": 2 * (AGG_ITERS + 1)}
        BASE = {n: sum(k for _, k in PASSES[:i]) for i, (n, _) in enumerate(PASSES)}
        EARLY = 20
        S_BASE = {n: K * i for i, n in enumerate(["l0", "l3"])}

        ROW_WIDTH = [3, 1, H]
        ROW_UNITS = [-(-KG * w // PERB) for w in ROW_WIDTH]
        ROW_BASE = [0, ROW_UNITS[0], ROW_UNITS[0] + ROW_UNITS[1]]
        steps3 = big[:, 6 * KP:9 * KP]

        def rows_buf(turn):
            w = ROW_WIDTH[turn]
            at = big.shape[1] - KG * P * w if turn == 0 else 0
            return big[:, at:at + KG * P * w]

        def rows_dst(turn):
            return [steps3, alpha0[:, :], qa[:, :]][turn]

        def bank(j, parts, cols, at=0):
            return PS[0:parts, j * BANK + at:j * BANK + at + cols]

        def agg_psum():
            return free(PS[0:NP, 0:1], [[D, NB], [1, D]])

        def packed(t, w):
            return free(t[0:NP, 0, 0:1], [[w, NB], [1, w]])

        def col(buf, j, w):
            return free(buf[:, 0:1], [[w, C]], j)

        D_UNITS = -(-3 * DG // PERB)

        SHARE = 6

        def share_psum(q, part, half):
            at = SHARE * half
            n = (CUTS[part + 1] - CUTS[part]) - at if half else SHARE
            return free(PS[0:NP, 0:1], [[2 * P, n], [NB, WN], [1, NB]], at * 2 * P + q * W)

        def share_sb(blk, part, half):
            at = SHARE * half
            n = (CUTS[part + 1] - CUTS[part]) - at if half else SHARE
            return free(blk[:, 0:1], [[WN, n], [1, WN], [NP, NB]], (CUTS[part] + at) * WN)

        block = ctx.enter_context(nc.Block())

        @block.sync
        def _(sp):
            src1, dst1, ety1, wt1 = (a.rearrange("(o e) -> o e", o=1) for a in (src, dst, etype, weight))
            sp.wait_ge(S["pads"], 1)
            for sb_t, dr in ((dst_i, dst1), (src_i, src1), (ety_i, ety1), (w_lin, wt1)):
                sp.dma_start(sb_t[0:FULL, :], dr[0, 0:FULL * C].rearrange("(p c) -> p c", c=C)).then_inc(S["edges_in"], 16)
                sp.dma_start(sb_t[FULL:P, 0:REST], dr[0:1, FULL * C:E]).then_inc(S["edges_in"], 16)
            sp.dma_start(prev_i[0:1, 1:C], dst1[0:1, 0:C - 1]).then_inc(S["edges_in"], 16)
            sp.dma_start(prev_i[1:FULL, :], dst1[0, C - 1:FULL * C - 1].rearrange("(p c) -> p c", c=C)).then_inc(S["edges_in"], 16)
            sp.dma_start(prev_i[FULL:P, 0:REST + 1], dst1[0:1, FULL * C - 1:E]).then_inc(S["edges_in"], 16)
            sp.dma_start(X[:], x.rearrange("(b p) f -> p b f", p=NP)).then_inc(S["x_in"], 16)
            for t, d in (
                (w1t_in[:], attn_w1.rearrange("(a i) j -> i a j", a=3)), (w2_col[:], attn_w2),
                (emb[:], emb_rel.rearrange("(g p) d -> p g d", g=2)), (rhs0[:, 0:D], loop_weight),
                (wm[:], W_msg), (wu_top[:], W_upd[0:D, :]), (wu_bot[:], W_upd[D:2 * D, :]),
                (bm_col[:], b_msg.rearrange("(p o) -> p o", o=1)), (watt[:], W_att), (w1_sb[:], W1),
                (b1_col[:], b1.rearrange("(p o) -> p o", o=1)), (w2_sb[:], W2),
            ):
                sp.dma_start(t, d).then_inc(S["weights_in"], 16)
            for j, v in enumerate((b_msg, b_upd, bias_att, b2, ln1_g, ln1_b, ln2_g, ln2_b)):
                sp.dma_start(vec[:, j, :], rows_on_all(v, P)).then_inc(S["vecs_in"], 16)
            sp.wait_ge(S["edges_ready"], 1)
            sp.dma_start(d_edges.rearrange("(p c) k -> p (c k)", p=P), big[:, 5 * C:8 * C]).then_inc(S["edges_out"], 16)
            sp.dma_start(d_dense.rearrange("(p c) k -> p (c k)", p=P), big[:, 8 * C:11 * C]).then_inc(S["dense_out"], 16)
            sp.wait_ge(S["zero_ready"], 1)
            for d in (d_fa0, d_fb0, d_fa3, d_fb3):
                flat = d.rearrange("e k -> (e k)")
                for j in range(d.shape[1]):
                    sp.dma_start(flat[j * EP:(j + 1) * EP].rearrange("(p c) -> p c", p=P), zrow[:]).then_inc(S["fills_zero"], 16)
            sp.wait_ge(S["pair_ready"], 1)
            sp.dma_start(d_pair.rearrange("(b p r) o -> p b (r o)", b=NB, p=NP),
                         free(big[0:NP, 0:1], [[RELS, NB], [1, RELS]])).then_inc(S["pair_out"], 16)
            sp.dma_start(d_h0.rearrange("(b p) f -> p b f", p=NP), Hn[:]).then_inc(S["tab_out"], 16)

            def linear_dmas(name, idx, width):
                n = LIN_TURN[name]
                for s in range(RING):
                    if BASE[name]:
                        sp.wait_ge(slot[s], 16 * BASE[name])
                if n:
                    sp.wait_ge(S["staged"], STAGED_BASE["l3"])
                for h in range(2):
                    sp.dma_start(idx_ring[:, HALF * h:HALF * h + HALF], idx[:, HALF * h:HALF * h + HALF]).then_inc(S[f"stage_in{h}"], 16)
                with sp.Fori(0, LIN_ITERS) as i:
                    for h in range(2):
                        for s in range(HALF * h, HALF * h + HALF):
                            sp.wait_ge(slot[s], 16 * i + 16 * (BASE[name] + 1))
                        sp.dma_start(qa[:, bass.ds((RING * i + HALF * h) * width, HALF * width)],
                                     free(ring[:, 0, 0:1], [[1, HALF * width]], HALF * width * h)).then_inc(S[f"q_out{h}"], 16)
                        sp.dma_start(idx_ring[:, HALF * h:HALF * h + HALF],
                                     idx[:, bass.ds(RING * i + (RING + HALF * h), HALF)]).then_inc(S[f"stage_in{h}"], 16)

            def softmax_dmas(turn, nh, lin, d_max, d_sum, d_fa, d_fb, d_al):
                w = nh * C
                sp.wait_ge(S["scan_ready"], 2 * turn + 1)
                sp.dma_start(d_max.rearrange("(p c) k -> p (c k)", p=P), lin).then_inc(S["scan_out"], 16)
                sp.wait_ge(S["fill_out"], 16 * NB * (2 * turn + 1))
                sp.dma_start(big[:, 0:2 * w], d_fa.rearrange("(p c) k -> p (c k)", p=P)).then_inc(S["fill_in"], 16)
                sp.wait_ge(S["scan_ready"], 2 * turn + 2)
                sp.dma_start(d_sum.rearrange("(p c) k -> p (c k)", p=P), big[:, 0:w]).then_inc(S["scan_out"], 16)
                sp.wait_ge(S["fill_out"], 16 * NB * (2 * turn + 2))
                sp.dma_start(big[:, w:2 * w], d_fb.rearrange("(p c) k -> p (c k)", p=P)).then_inc(S["fill_in"], 16)
                sp.wait_ge(S["alpha_ready"], turn + 1)
                sp.dma_start(d_al.rearrange("(p c) k -> p (c k)", p=P), qa[:, 0:w]).then_inc(S["alpha_out"], 16)

            linear_dmas("pair", idx_pair, 1)
            softmax_dmas(0, 1, big[:, 0:C], d_max0, d_sum0, d_fa0, d_fb0, d_al0)
            sp.wait_ge(S["blk_out"], 32 * NB)
            sp.wait_ge(S["rows_sb"], ROW_BASE[1] + ROW_UNITS[1])
            for turn, d_blk in enumerate((d_cnt, d_wgt, d_wgt)):
                n0, nb = turn * NB, BB
                if turn:
                    sp.wait_ge(S["blk_used"], n0)
                    sp.wait_ge(S["ct_used"], 7 * (NB + 1))
                for b in range(nb):
                    sp.dma_start(blk_in[:, b, :], d_blk[b]).then_inc(S[f"blk_in{b}"], 16)
                with sp.Fori(0, (NB - 1) // nb - 1) as i:
                    for b in range(nb):
                        sp.wait_ge(S["blk_used"], nb * i + (n0 + b + 1))
                        sp.dma_start(blk_in[:, b, :], d_blk[bass.ds(nb * i + (b + nb), 1)].rearrange("o p m -> p (o m)")).then_inc(S[f"blk_in{b}"], 16)
                sp.wait_ge(S["blk_used"], n0 + NB - nb)
                sp.dma_start(blk_in[:, 0, :], d_blk[NB - 1]).then_inc(S["blk_in0"], 16)
            for j, v in enumerate((att_src, att_dst)):
                if j == 0:
                    sp.wait_ge(S["blk_used"], 3 * NB)
                sp.dma_start(att_b[:, j, :], rows_on_all(v, D)).then_inc(S["watt_in"], 16)
            sp.wait_ge(S["y_sb"], NB)
            y_dram = d_y.rearrange("(b p) m -> p b m", p=NP)
            sp.dma_start(y_dram, big[0:NP, :].rearrange("p (b m) -> p b m", b=NB)).then_inc(S["y_out"], 16)
            softmax_dmas(1, H, big[:, 0:H * C], d_max3, d_sum3, d_fa3, d_fb3, d_al3)
            sp.wait_ge(S["ring_used"], USED_BASE["l3"] + K + RING)
            sp.dma_start(big[0:NP, :].rearrange("p (b m) -> p b m", b=NB), y_dram).then_inc(S["y_back"], 16)
            sp.wait_ge(S["x_done"], 1)
            sp.dma_start(out.rearrange("(b p) f -> p b f", p=NP), X[:]).then_inc(S["out_done"], 16)
            sp.wait_ge(S["out_done"], 16)

        @block.gpsimd
        def _(pool):
            nc.gpsimd.memset(dst_i[:, :], E)
            nc.gpsimd.memset(prev_i[:, :], E)
            nc.gpsimd.memset(src_i[:, :], 0)
            nc.gpsimd.memset(ety_i[:, :], 0)
            nc.gpsimd.memset(w_lin[:, :], 0.0).then_inc(S["pads"], 1)
            nc.gpsimd.memset(zrow[:], 0.0).then_inc(S["zero_ready"], 1)
            nc.gpsimd.memset(zero_bf[:], 0.0)
            nc.gpsimd.memset(ones[:], 1.0)
            nc.gpsimd.memset(ident[:], 0.0)
            nc.gpsimd.memset(sel5[:], 0.0)
            nc.gpsimd.memset(tri[:], 1.0).then_inc(S["preinc"], 1)
            pool.wait_ge(S["preinc"], 1)
            nc.gpsimd.affine_select(out=ident[:], in_=ident[:], compare_op=ALU.not_equal, fill=1.0,
                                    base=0, pattern=[[-1, P]], channel_multiplier=1)
            nc.gpsimd.affine_select(out=tri[:], in_=tri[:], compare_op=ALU.is_gt, fill=0.0,
                                    base=0, pattern=[[1, NP]], channel_multiplier=-1)
            nc.gpsimd.affine_select(out=sel5[:], in_=sel5[:], compare_op=ALU.not_equal, fill=1.0,
                                    base=0, pattern=[[-WN, WB]], channel_multiplier=1)
            nc.gpsimd.iota(kg5_i[:], [[P, DG]], base=0, channel_multiplier=1)
            nc.gpsimd.iota(kg_i[:], [[P, KG]], base=0, channel_multiplier=1)
            nc.gpsimd.iota(iota_i[:], [[1, KP]], base=0, channel_multiplier=0).then_inc(S["consts"], 1)
            pool.sem_inc(S["ring_used"], RING)
            pool.sem_inc(S["hist_used"], RING)
            pool.sem_inc(S["one_used"], UD)
            pool.sem_inc(S["ct_sb"], 4)
            pool.sem_inc(S["ct_used"], 7)
            pool.sem_inc(S["neigh_sb"], BB)
            for name in ("look_tr", "look_t", "look_mm", "look_used"):
                pool.sem_inc(S[name], 2)
            pool.sem_inc(S["look_sum"], 1)

            def gather(table, into, s):
                pool.indirect_dma_start(into[:, s, :], None, table,
                                        bass.IndirectOffsetOnAxis(ap=idx_ring[:, s:s + 1], axis=0)).then_inc(slot[s], 16)

            def linear_pass(name, table, into, first=0, end=LIN_ITERS):
                n = LIN_TURN[name]

                def turn(i, fresh):
                    for h in range(2):
                        pool.wait_ge(S[f"stage_in{h}"], 16 * i + 16 * (n * (LIN_ITERS + 1) + 1))
                        if not fresh:
                            pool.wait_ge(S[f"q_out{h}"], 16 * i + 16 * n * LIN_ITERS)
                            pool.sem_inc(S["halves_begun"], 1)
                        for s in range(HALF * h, HALF * h + HALF):
                            gather(table, into, s)

                if first == 0:
                    turn(0, n == 0)
                with pool.Fori(max(first, 1), end) as i:
                    turn(i, False)

            def gather_pass(name, table, into):
                used, sbase = USED_BASE[name], STAGED_BASE[name]
                with pool.Fori(0, AGG_ITERS) as i:
                    for h in range(2):
                        pool.wait_ge(S["staged"], 2 * i + (sbase + h + 1))
                        pool.wait_ge(S["ring_used"], RING * i + (used + HALF * (h + 1)))
                        pool.sem_inc(S["halves_begun"], 1)
                        for s in range(HALF * h, HALF * h + HALF):
                            gather(table, into, s)

            def row_gather(turn, d):
                w = ROW_WIDTH[turn]
                buf = rows_buf(turn)
                table = d.rearrange("(t e) k -> t (e k)", e=P)
                for g in range(KG):
                    pool.indirect_dma_start(buf[:, g * P * w:(g + 1) * P * w], None, table,
                                            bass.IndirectOffsetOnAxis(ap=tk_i[:, g:g + 1], axis=0)).then_inc(S["rows_in"], 16)

            def from_segments(table, into, w):
                into = packed(into, w)
                for b in range(NB):
                    pool.indirect_dma_start(into[:, b, :], None, table,
                                            bass.IndirectOffsetOnAxis(ap=last_i[:, b:b + 1], axis=0),
                                            bounds_check=EP - 1, oob_is_err=False).then_inc(S["nodes_in"], 16)

            def to_segments(table, w):
                vals = packed(nfill, w)
                for b in range(NB):
                    pool.indirect_dma_start(table, bass.IndirectOffsetOnAxis(ap=start_i[:, b:b + 1], axis=0),
                                            vals[:, b, :], None,
                                            bounds_check=EP - 1, oob_is_err=False).then_inc(S["fill_out"], 16)

            def softmax_nodes(turn, nh, d_max, d_sum, d_fa, d_fb, d_al):
                pool.wait_ge(S["nmx_ready"], turn + 1)
                pool.wait_ge(S["scan_out"], 16 * (2 * turn + 1))
                from_segments(d_max, nmx, nh)
                pool.wait_ge(S["fill_ready"], 2 * turn + 1)
                to_segments(d_fa, 2 * nh)
                pool.wait_ge(S["scan_out"], 16 * (2 * turn + 2))
                from_segments(d_sum, nden, nh)
                pool.wait_ge(S["fill_ready"], 2 * turn + 2)
                to_segments(d_fb, nh)
                pool.wait_ge(S["alpha_out"], 16 * (turn + 1))
                row_gather(turn + 1, d_al)

            pool.wait_ge(S["tk_ready"], 1)
            pool.wait_ge(S["edges_out"], 16)
            row_gather(0, d_edges)
            pool.wait_ge(S["pair_out"], 16)
            pair_ring = free(ring[:, 0, 0:1], [[1, RING], [1, 1]])
            linear_pass("pair", d_pair, pair_ring, end=EARLY)
            pool.wait_ge(S["k5_ready"], 1)
            pool.wait_ge(S["dense_out"], 16)
            dense_rows = d_dense.rearrange("(t e) k -> t (e k)", e=P)
            for g in range(DG):
                pool.indirect_dma_start(drow[:, g * 3 * P:(g + 1) * 3 * P], None, dense_rows,
                                        bass.IndirectOffsetOnAxis(ap=tk5_i[:, g:g + 1], axis=0)).then_inc(S["drows_in"], 16)
            linear_pass("pair", d_pair, pair_ring, first=EARLY)
            pool.wait_ge(S["idx_ready"], 1)
            pool.wait_ge(S["fills_zero"], 16 * (2 + 1 + 2 * H + H))
            softmax_nodes(0, 1, d_max0, d_sum0, d_fa0, d_fb0, d_al0)
            pool.wait_ge(S["tab_out"], 16)
            gather_pass("l0", d_h0, ring)
            pool.wait_ge(S["y_out"], 16)
            softmax_nodes(1, H, d_max3, d_sum3, d_fa3, d_fb3, d_al3)
            gather_pass("l3", d_y, yring)

        @block.scalar
        def _(act):
            def root(turn):
                act.wait_ge(S["ln_var"], turn + 1)
                nc.scalar.activation(st[:, 2, :], st[:, 1, :], ACT.Sqrt).then_inc(S["ln_root"], 1)

            def turned(turn):
                act.wait_ge(S["ht_psum"], turn + 1)
                for j in range(-(-NB // PERB)):
                    n = min(PERB, NB - PERB * j)
                    last = nc.scalar.activation(
                        HT[:, PERB * j:PERB * j + n, :],
                        bank(j, D, PERB * P).rearrange("p (n c) -> p n c", c=P)[:, 0:n, 0:NP], ACT.Copy)
                last.then_inc(S["ht_sb"], 1)

            def stage(idx, i, h):
                nc.scalar.activation(idx_ring[:, HALF * h:HALF * h + HALF],
                                     idx[:, bass.ds(RING * i + HALF * h, HALF)], ACT.Copy).then_inc(S["staged"], 1)

            def index_pass(name, idx):
                base = BASE[name]
                if name == "l3":
                    act.wait_ge(S["staged"], STAGED_BASE[name])
                for h in range(2):
                    act.wait_ge(S[f"stage_in{h}"], 16 * (LIN_ITERS + 1))
                    act.wait_ge(S[f"q_out{h}"], 16 * LIN_ITERS)
                for s in range(RING):
                    act.wait_ge(slot[s], 16 * base)
                for h in range(2):
                    stage(idx, 0, h)
                with act.Fori(0, ITERS[name]) as i:
                    for h in range(2):
                        for s in range(HALF * h, HALF * h + HALF):
                            act.wait_ge(slot[s], 16 * i + 16 * (base + 1))
                        nc.scalar.activation(idx_ring[:, HALF * h:HALF * h + HALF],
                                             idx[:, bass.ds(RING * i + (RING + HALF * h), HALF)],
                                             ACT.Copy).then_inc(S["staged"], 1)

            def rows_out(turn):
                w, dst = ROW_WIDTH[turn], rows_dst(turn)
                for u in range(ROW_UNITS[turn]):
                    act.wait_ge(S["rows_tr"], ROW_BASE[turn] + u + 1)
                    n = min(PERB, KG * w - PERB * u) * P
                    nc.scalar.activation(dst[:, u * BANK:u * BANK + n], bank(u % 8, P, n), ACT.Copy).then_inc(S["rows_sb"], 1)

            root(0)
            turned(0)
            act.wait_ge(S["dense_out"], 16)
            rows_out(0)
            act.wait_ge(S["fills_zero"], 16 * (2 + 1 + 2 * H + H))
            for u in range(D_UNITS):
                act.wait_ge(S["drows_tr"], u + 1)
                n = min(PERB, 3 * DG - PERB * u) * P
                nc.scalar.activation(dcols[:, u * BANK:u * BANK + n], bank(u % 8, P, n), ACT.Copy).then_inc(S["drows_sb"], 1)
            act.wait_ge(S["kpos_sb"], 1)
            act.dma_start(d_pos, pos_c[:]).then_inc(S["pos_out"], 16)
            act.wait_ge(S["pos_out"], 16)
            act.dma_start(pos_i[:], d_pos.rearrange("(o g) p -> o (g p)", o=1)).then_inc(S["pos_in"], 16)

            def block_out(b, first):
                for part in range(2):
                    end = act.value_load(cut_i[0:1, bass.ds(2 * b + (part + 1), 1)], min_val=0, max_val=KD)
                    act.wait_ge(S["one_used"], end + UD)
                    if part == 0 and not first:
                        act.wait_ge(S["blk_out"], 32 * b)
                    nc.scalar.activation(share_sb(blk_c, part, 0), share_psum(0, part, 0), ACT.Copy)
                    nc.scalar.activation(share_sb(blk_w, part, 0), share_psum(1, part, 0), ACT.Copy).then_inc(S["share0_sb"], 1)
                act.wait_ge(S["share0_sb"], 2 * b + 2)
                act.wait_ge(S["share1_sb"], 2 * b + 2)
                act.dma_start(d_cnt[bass.ds(b, 1)].rearrange("o p m -> p (o m)"), blk_c).then_inc(S["blk_out"], 16)
                act.dma_start(d_wgt[bass.ds(b, 1)].rearrange("o p m -> p (o m)"), blk_w).then_inc(S["blk_out"], 16)

            act.wait_ge(S["dense_ready"], 1)
            block_out(0, True)
            with act.Fori(1, NB) as b:
                block_out(b, False)
            act.wait_ge(S["exp_in"], 1)
            nc.scalar.activation(qa[:, 0:C], qa[:, 0:C], ACT.Exp).then_inc(S["exp_done"], 1)
            rows_out(1)
            index_pass("l0", idx_src_k)
            root(1)
            turned(1)

            def counts_out(q0):
                for g in range(7):
                    n = min(PERB, NB - PERB * g)
                    act.wait_ge(S["ct_tr"], q0 + (g + 1))
                    act.wait_ge(S["ct_used"], q0 + (g + 1))
                    nc.scalar.activation(blk_t[:, PERB * g:PERB * g + n, 0:NP],
                                         bank(4 + g % 4, NP, PERB * P).rearrange("p (n c) -> p n c", c=P)[:, 0:n, 0:NP],
                                         ACT.Copy).then_inc(S["ct_sb"], 1)

            def target_rows(n, j):
                if j == 0:
                    act.wait_ge(S["tab_ready"], 1)
                nc.scalar.activation(t_row[:, j, :], T1[:, bass.ds(n, 1), :].rearrange("p a f -> p (a f)"), ACT.Copy)

            with act.Fori(0, (NB - 1) // BB) as i:
                for j in range(BB):
                    target_rows(BB * i + j, j)
                    counts_out(7 * BB * i + 7 * j)
            target_rows(NB - 1, 0)
            counts_out(7 * (NB - 1))
            root(2)
            root(3)

            def sums_out(turn, n, j):
                act.wait_ge(S["blk_used"], n + (turn * NB + 1))
                nc.scalar.activation(HT[:, bass.ds(n, 1), :].rearrange("p a f -> p (a f)"), bank(4 + j, D, NP),
                                     ACT.Copy).then_inc(S["neigh_sb"], 1)

            for turn in (1, 2):
                if turn == 2:
                    act.wait_ge(S["tab_ready"], 3)
                with act.Fori(0, (NB - 1) // BB) as i:
                    for j in range(BB):
                        sums_out(turn, BB * i + j, j)
                sums_out(turn, NB - 1, 0)
            root(4)
            turned(2)
            for b in range(NB):
                act.wait_ge(S["y_bank"], b + 1)
                nc.scalar.activation(big[0:NP, b * HD:(b + 1) * HD], bank(b % 7, NP, HD), ACT.Copy).then_inc(S["y_sb"], 1)

            def turned_hots(j, g):
                act.wait_ge(S["look_tr"], g + (1 + 2))
                act.wait_ge(S["look_mm"], g + 1)
                nc.scalar.activation(look_t[0:NP, j, :], bank(4 + j, NP, CB * P), ACT.Copy).then_inc(S["look_t"], 1)

            with act.Fori(0, LOOK_GROUPS // 2) as i:
                for j in range(2):
                    turned_hots(j, 2 * i + j)
            act.wait_ge(S["exp_in"], 2)
            nc.scalar.activation(packed(nself, H), packed(nself, H), ACT.Exp)
            nc.scalar.activation(qa[:, 0:H * C], qa[:, 0:H * C], ACT.Exp).then_inc(S["exp_done"], 1)
            rows_out(2)
            index_pass("l3", idx_src_k)
            root(5)
            turned(3)
            act.wait_ge(S["ff1"], 1)
            for j in range(-(-N // 500)):
                n = min(500, N - 500 * j)
                last = nc.scalar.activation(big[:, 500 * j:500 * j + n], bank(j, P, n), ACT.Relu, bias=b1_col[:, 0:1])
            last.then_inc(S["ff1_sb"], 1)
            root(6)

        @block.tensor
        def _(pe):
            def turn_nodes(turn):
                pe.wait_ge(S["h_ready"], turn + 1)
                for b in range(NB):
                    last = nc.tensor.transpose(bank(b // PERB, D, NP, (b % PERB) * P), Hn[:, b, :], ident[0:NP, 0:NP])
                last.then_inc(S["ht_psum"], 1)
                pe.wait_ge(S["ht_sb"], turn + 1)

            def turn_rows(turn):
                w, buf = ROW_WIDTH[turn], rows_buf(turn)
                pe.wait_ge(S["rows_in"], 16 * KG * (turn + 1))
                for u in range(ROW_UNITS[turn]):
                    if u >= 8:
                        pe.wait_ge(S["rows_sb"], ROW_BASE[turn] + u - 7)
                    for q in range(PERB * u, min(PERB * u + PERB, KG * w)):
                        h, g = q // KG, q % KG
                        last = nc.tensor.transpose(bank(u % 8, P, P, (q % PERB) * P),
                                                   free(buf[:, 0:1], [[w, P]], g * P * w + h), ident[:])
                    last.then_inc(S["rows_tr"], 1)

            def zero_banks(first, n, parts=NP):
                for j in range(first, first + n):
                    nc.tensor.matmul(bank(j, parts, BANK), zero_bf[:, 0:parts], zero_bf[:], start=True, stop=True)

            def load_blocks(i):
                return nc.values_load_multi_w_load_instructions(
                    bk_i[0:1, bass.ds(RING * i, RING)], engines=[mybir.EngineType.PE], min_val=0, max_val=NB - 1,
                    skip_runtime_bounds_check_because="a step's block is a count of at most NB - 1 offsets")[1]

            def agg_pass(name):
                base, ob = BASE[name], S_BASE[name]
                zero_banks(0, 4 if name == "l0" else 7)
                with pe.Fori(0, AGG_ITERS) as i:
                    blocks = load_blocks(i)
                    for s in range(RING):
                        pe.wait_ge(slot[s], 16 * i + 16 * (base + 1))
                        if name == "l0":
                            pe.wait_ge(S["s_ready"], RING * i + (ob + s + 1))
                        elif s % MB == 0:
                            pe.wait_ge(S["s_ready"], RING * i + (ob + s + MB))
                        if name == "l3":
                            for j in range(2):
                                mm = nc.tensor.matmul(PS[0:NP, bass.ds(blocks[s] * (2 * D), 2 * D)], s_ring[:, s, 0:NP],
                                                      prod[:, s % PR, j * 2 * D:(j + 1) * 2 * D], start=False, stop=False, skip_group_check=True)
                        else:
                            mm = nc.tensor.matmul(PS[0:NP, bass.ds(blocks[s] * D, D)], s_ring[:, s, 0:NP],
                                                  ring[:, s, :], start=False, stop=False, skip_group_check=True)
                        if name == "l0":
                            mm.then_inc(S["ring_used"], 1)
                        elif s % MB == MB - 1:
                            mm.then_inc(S["ring_used"], MB)

            pe.wait_ge(S["consts"], 1)
            pe.wait_ge(S["cnt_ready"], 1)
            nc.tensor.transpose(bank(4, 2 * H, P), chain_in[:], ident[:])
            nc.tensor.matmul(bank(3, P, NB + 1), ones[:], cnt[:], start=True, stop=True).then_inc(S["chain_tr"], 1)
            pe.wait_ge(S["weights_in"], 16 * 12)
            for j in range(3):
                nc.tensor.transpose(bank(0, D, D, j * D), w1t_in[:, j, :], ident[0:D, 0:D])
            for g in range(2):
                mm = nc.tensor.transpose(bank(1, D, RELS // 2, g * RELS // 2), emb[:, g, :], ident[0:RELS // 2, 0:RELS // 2])
            nc.tensor.transpose(bank(5, D, D), wm[:], ident[0:D, 0:D]).then_inc(S["wtr"], 1)
            pe.wait_ge(S["wtr_sb"], 1)
            nc.tensor.matmul(bank(2, D, D, P), wmT[:], wu_bot[:], start=True, stop=True)
            nc.tensor.matmul(bank(2, P, D, 2 * P), bm_b[:], wu_bot[:], start=True, stop=True)
            for j in range(3):
                mm = nc.tensor.matmul(bank(2, D, 1, j), w1T[:, j * D:(j + 1) * D], w2_col[:], start=True, stop=True)
            mm.then_inc(S["vproj"], 1)
            turn_nodes(0)
            nc.tensor.matmul(bank(7, NP, RELS), vr_b[:, 0:NP], embT[:], start=True, stop=True)
            for b in range(NB):
                mm = nc.tensor.matmul(bank(b // PERB, NP, D + 2, (b % PERB) * P), HT[:, b, :], rhs0[:], start=True, stop=True)
            mm.then_inc(S["node_mm"], 1)
            pe.wait_ge(S["pair_ready"], 1)
            turn_rows(0)
            pe.wait_ge(S["rows_sb"], ROW_UNITS[0])
            zero_banks(7, 1)
            pe.wait_ge(S["steps_ready"], 1)
            with pe.Fori(0, AGG_ITERS) as i:
                blocks = load_blocks(i)
                for s in range(RING):
                    if s % HALF == 0:
                        pe.wait_ge(S["hist_s"], RING * i + s + HALF)
                    mm = nc.tensor.matmul(PS[0:NP, bass.ds(blocks[s] * 4 + 7 * BANK, 4)],
                                          free(s_bf[:, 0:1], [[HALF, NP]], s // HALF * W * HALF + s % HALF),
                                          w4[:, bass.ds(RING * i + s, 1), :].rearrange("p a b -> p (a b)"),
                                          start=False, stop=False, skip_group_check=True)
                    if s % HALF == HALF - 1:
                        mm.then_inc(S["hist_used"], HALF)
            pe.wait_ge(S["tri_in"], 1)
            nc.tensor.matmul(bank(6, NP, NB), tri[:], deg[:], start=True, stop=True).then_inc(S["tri_done"], 1)

            pe.wait_ge(S["rank_in"], 1)
            nc.tensor.matmul(bank(0, P, NW // 2), ones[0:NP, :], rank_in[:, 0:NW // 2], start=True, stop=True)
            nc.tensor.matmul(bank(1, P, NW - NW // 2), ones[0:NP, :], rank_in[:, NW // 2:NW], start=True, stop=True).then_inc(S["r5_tr"], 1)
            pe.wait_ge(S["drows_in"], 16 * DG)
            pe.wait_ge(S["k5_ready"], 2)
            for u in range(D_UNITS):
                if u >= 8:
                    pe.wait_ge(S["drows_sb"], u - 7)
                for q in range(PERB * u, min(PERB * u + PERB, 3 * DG)):
                    h, g = q // DG, q % DG
                    last = nc.tensor.transpose(bank(u % 8, P, P, (q % PERB) * P), free(drow[:, 0:1], [[3, P]], g * 3 * P + h), ident[:])
                last.then_inc(S["drows_tr"], 1)
            pe.wait_ge(S["drows_sb"], D_UNITS)
            nc.tensor.transpose(bank(7, DG, P), k5[:, 5, :], ident[:]).then_inc(S["kpos_tr"], 1)

            def dense_block(b, first):
                for part in range(2):
                    at = [pe.value_load(cut_i[0:1, bass.ds(2 * b + (part + j), 1)], min_val=0, max_val=KD) for j in range(2)]
                    if part or not first:
                        pe.wait_ge(S["share0_sb"], 2 * b + part)
                        pe.wait_ge(S["share1_sb"], 2 * b + part)
                    for j in range(7):
                        nc.tensor.matmul(bank(j, P, 2), zero_bf[:, 0:P], zero_bf[:, 0:2], start=True, stop=True)
                    with pe.Fori(at[0], at[1], UD) as k:
                        pos = nc.values_load_multi_w_load_instructions(
                            pos_i[0:1, bass.ds(k, UD)], engines=[mybir.EngineType.PE], min_val=0, max_val=CUTS[1] - 1,
                            skip_runtime_bounds_check_because="a window's place is below a part's size")[1]
                        for s in range(UD):
                            if s % QB == 0:
                                pe.wait_ge(S["one_ready"], k + (s + QB))
                            lhs = free(hot_step(s // QB, s % QB, 0, 1), [[QB, NP]])
                            for q, n, to in ((1, 2, 0), (3, 1, W), (4, 1, W)):
                                mm = nc.tensor.matmul(PS[0:NP, bass.ds(pos[s] * (2 * P) + to, n * W)], lhs, hot_step(s // QB, s % QB, q, n),
                                                      start=False, stop=False, skip_group_check=True)
                            if s % QB == QB - 1:
                                mm.then_inc(S["one_used"], QB)

            pe.wait_ge(S["dense_ready"], 1)
            pe.wait_ge(S["pos_in"], 16)
            dense_block(0, True)
            with pe.Fori(1, NB) as b:
                dense_block(b, False)
            pe.wait_ge(S["share0_sb"], 2 * NB)
            pe.wait_ge(S["share1_sb"], 2 * NB)

            chains = [0]

            def chain(w):
                n = chains[0]
                pe.wait_ge(S["ends_ready"], n + 1)
                nc.tensor.transpose(bank(5, w, P), ends[:, 0:w], ident[:]).then_inc(S["ends_tr"], 1)
                pe.wait_ge(S["carry_in"], n + 1)
                nc.tensor.transpose(bank(6, P, w), carry_row[0:w, 0:P], ident[0:w, 0:w]).then_inc(S["carry_tr"], 1)
                chains[0] += 1

            for w in (1, 2, 1, 1):
                chain(w)
            turn_rows(1)
            pe.wait_ge(S["rows_sb"], ROW_BASE[1] + ROW_UNITS[1])
            agg_pass("l0")
            turn_nodes(1)
            for b in range(NB):
                mm = nc.tensor.matmul(bank(0, NP, D, b * D), HT[:, b, :], wmu[:], start=True, stop=True)
            mm.then_inc(S["node_mm"], 1)
            pe.wait_ge(S["tab_ready"], 1)
            zero_banks(0, 4)
            for b in range(NB):
                nc.tensor.matmul(bank(0, NP, D, b * D), HT[:, b, :], wu_top[:], start=False, stop=False, skip_group_check=True)

            def count_block(n, slot_no, i):
                pe.wait_ge(S[f"blk_in{slot_no}"], 16 * i + 16)

                def product(g):
                    pe.wait_ge(S["ct_sb"], 7 * n + (g + 5))
                    for hi in range(PERB * g, min(PERB * g + PERB, NB)):
                        mm = nc.tensor.matmul(bank(0, NP, D, hi * D), blk_t[:, hi, 0:NP],
                                              t_row[:, slot_no, :],
                                              start=False, stop=False, skip_group_check=True)
                    mm.then_inc(S["ct_used"], 1)

                for g in range(7):
                    pe.wait_ge(S["ct_sb"], 7 * n + (g + 1))
                    for hi in range(PERB * g, min(PERB * g + PERB, NB)):
                        tr = nc.tensor.transpose(bank(4 + g % 4, NP, NP, (hi % PERB) * P),
                                                 blk_in[:, slot_no, hi * NP:(hi + 1) * NP], ident[0:NP, 0:NP])
                    tr.then_inc(S["ct_tr"], 1)
                    if g >= 2:
                        product(g - 2)
                nc.tensor.matmul(bank(7, 2, 2, 508), zero_bf[:, 0:2], zero_bf[:, 0:2], start=True, stop=True).then_inc(S["blk_used"], 1)
                product(5)
                product(6)

            with pe.Fori(0, (NB - 1) // BB) as i:
                for j in range(BB):
                    count_block(BB * i + j, j, i)
            count_block(NB - 1, 0, (NB - 1) // BB)
            for turn in (1, 2):
                pe.wait_ge(S["tab_ready"], turn + 1)

                def weight_block(n, slot_no, i):
                    pe.wait_ge(S[f"blk_in{slot_no}"], 16 * i + 16 * (loads_before(turn, slot_no) + 1))
                    pe.wait_ge(S["neigh_sb"], n + ((turn - 1) * NB + 1))
                    for hi in range(NB):
                        mm = nc.tensor.matmul(bank(4 + slot_no, D, NP), T1[:, hi, :], blk_in[:, slot_no, hi * NP:(hi + 1) * NP],
                                              start=(hi == 0), stop=(hi == NB - 1), skip_group_check=True)
                    mm.then_inc(S["blk_used"], 1)

                nb = BB
                with pe.Fori(0, (NB - 1) // nb) as i:
                    for j in range(nb):
                        weight_block(nb * i + j, j, i)
                weight_block(NB - 1, 0, (NB - 1) // nb)
                pe.wait_ge(S["neigh_sb"], turn * NB + BB)
                for b in range(NB):
                    last = nc.tensor.transpose(bank(0, NP, D, b * D), HT[:, b, :], ident[0:D, 0:D])
                last.then_inc(S["neigh_tr"], 1)
            turn_nodes(2)
            pe.wait_ge(S["wasd_ready"], 1)
            for b in range(NB):
                mm = nc.tensor.matmul(bank(7, NP, 2 * H, b * 2 * H), HT[:, b, :], w_asd[:], start=True, stop=True)
            mm.then_inc(S["node_mm"], 1)
            for b in range(NB):
                if b >= 7:
                    pe.wait_ge(S["y_sb"], b - 6)
                nc.tensor.matmul(bank(b % 7, NP, HD), HT[:, b, :], watt[:], start=True, stop=True).then_inc(S["y_bank"], 1)
            pe.wait_ge(S["y_sb"], NB)

            def turn_hots(j, g):
                pe.wait_ge(S["look_hot"], g + 1)
                pe.wait_ge(S["look_t"], g + 1)
                for s in range(CB):
                    mm = nc.tensor.matmul(bank(4 + j, NP, P, s * P), free(look_hot[:, 0:1], [[CB, NP]], j * CB * W + s), ident_bf,
                                          start=True, stop=True)
                mm.then_inc(S["look_tr"], 1)

            def look_up(j, g):
                pe.wait_ge(S["look_t"], g + (1 + 2))
                pe.wait_ge(S["look_used"], g + 1)
                for s in range(CB):
                    for r in range(3):
                        mm = nc.tensor.matmul(bank(2 * j, P, HN, s * (BANK // 2)), look_t[0:NP, j, s * P:(s + 1) * P],
                                              src_parts[:, r * HN:(r + 1) * HN], start=(r == 0), stop=(r == 2), skip_group_check=True)
                mm.then_inc(S["look_mm"], 1)

            turn_hots(0, 0)
            with pe.Fori(0, LOOK_GROUPS // 2 - 1) as i:
                for j in range(2):
                    turn_hots(1 - j, 2 * i + (j + 1))
                    look_up(j, 2 * i + j)
            turn_hots(1, LOOK_GROUPS - 1)
            look_up(0, LOOK_GROUPS - 2)
            look_up(1, LOOK_GROUPS - 1)
            for w in (H, 2 * H, H, H):
                chain(w)
            turn_rows(2)
            pe.wait_ge(S["rows_sb"], ROW_BASE[2] + ROW_UNITS[2])
            agg_pass("l3")
            turn_nodes(3)
            for j in range(-(-N // 500)):
                n = min(500, N - 500 * j)
                mm = nc.tensor.matmul(bank(j, P, n), w1_sb[:], free(HT[:, 0, 0:1], [[1, n]], 500 * j), start=True, stop=True)
            mm.then_inc(S["ff1"], 1)
            pe.wait_ge(S["ff1_sb"], 1)
            for b in range(NB):
                mm = nc.tensor.matmul(bank(0, NP, D, b * D), big[:, b * NP:(b + 1) * NP], w2_sb[:], start=True, stop=True)
            mm.then_inc(S["node_mm"], 1)

        @block.vector
        def _(v):
            v_ = nc.vector
            done = [0]

            def go(ins, wait=True):
                done[0] += 1
                ins.then_inc(S["dve"], 1)
                if wait:
                    v.wait_ge(S["dve"], done[0])

            def mark(name):
                v.wait_ge(S["dve"], done[0])
                v.sem_inc(S[name], 1)

            def bc(t, n):
                return free(t, [list(t.ap[1]), [0, n]])

            def vb(j):
                return free(vec[0:NP, j, 0:1], [[0, NB], [1, D]])

            roots = [0]

            def layer_norm(src_t, dst_t):
                go(v_.tensor_reduce(st[:, 0, :], src_t, AX_X, ALU.add))
                go(v_.tensor_scalar(st[:, 0, :], st[:, 0, :], 1.0 / D, None, ALU.mult))
                go(v_.tensor_tensor(T1[:], src_t, bc(st[:, 0, :], D), ALU.subtract))
                go(v_.tensor_tensor(dst_t, T1[:], T1[:], ALU.mult))
                go(v_.tensor_reduce(st[:, 1, :], dst_t, AX_X, ALU.add))
                go(v_.tensor_scalar(st[:, 1, :], st[:, 1, :], 1.0 / D, LN_EPS, ALU.mult, ALU.add))
                inv_root()
                go(v_.tensor_tensor(dst_t, T1[:], bc(st[:, 3, :], D), ALU.mult))

            def inv_root():
                mark("ln_var")
                roots[0] += 1
                v.wait_ge(S["ln_root"], roots[0])
                go(v_.reciprocal(st[:, 3, :], st[:, 2, :]))
                go(v_.tensor_tensor(st[:, 2, :], st[:, 3, :], st[:, 3, :], ALU.mult))
                go(v_.tensor_tensor(st[:, 2, :], st[:, 2, :], st[:, 1, :], ALU.mult))
                go(v_.tensor_scalar(st[:, 2, :], st[:, 2, :], -0.5, 1.5, ALU.mult, ALU.add))
                go(v_.tensor_tensor(st[:, 3, :], st[:, 3, :], st[:, 2, :], ALU.mult))

            v.wait_ge(S["consts"], 1)
            go(v_.tensor_copy(iota_row[:], iota_i[:]))
            go(v_.tensor_copy(iota_bf[:], iota_i[:, 0:NP + 1]))
            go(v_.tensor_copy(tk2[:], kg_i[:]))
            go(v_.memset(idx_pair[:, C:C + RING], 0))
            go(v_.memset(idx_src_k[:, KP:KP + RING], 0))
            go(v_.memset(s_ring[:], 0.0))
            v.wait_ge(S["edges_in"], 16 * 11)
            dstf, prevf = junk[:, 0:C], negst
            go(v_.tensor_copy(dstf, dst_i))
            go(v_.tensor_copy(edge_lin[:, :, 1], src_i))
            go(v_.tensor_copy(edge_lin[:, :, 2], w_lin))
            go(v_.tensor_copy(notst[:], ety_i))
            go(v_.tensor_copy(edge_lin[:, :, 0], dstf))
            go(v_.scalar_tensor_tensor(idx_pair[:, 0:C], edge_lin[:, :, 1], float(RELS), notst[:], ALU.mult, ALU.add))
            hi_f, lo_f = negst[:], idx_f[:, 0:C]
            q_i = idx_f[:, 0:C].bitcast(I32)
            go(v_.tensor_scalar(hi_f, edge_lin[:, :, 1], 0.5, 1.0 / NP, ALU.add, ALU.mult))
            go(v_.tensor_scalar(q_i, hi_f, 0.5, None, ALU.subtract))
            go(v_.tensor_copy(hi_f, q_i))
            go(v_.scalar_tensor_tensor(lo_f, hi_f, -float(NP), edge_lin[:, :, 1], ALU.mult, ALU.add))
            for op, sign in ((ALU.is_ge, 1.0), (ALU.is_lt, -1.0)):
                go(v_.tensor_scalar(notst[:], lo_f, float(NP) if sign > 0 else 0.0, sign, op, ALU.mult))
                go(v_.tensor_tensor(hi_f, hi_f, notst[:], ALU.add))
                go(v_.scalar_tensor_tensor(lo_f, notst[:], -float(NP), lo_f, ALU.mult, ALU.add))
            go(v_.tensor_copy(dense_lin[:, :, 0], lo_f))
            go(v_.tensor_copy(lo_b[:], lo_f))
            go(v_.tensor_copy(hi_b[:], hi_f))
            go(v_.scalar_tensor_tensor(dense_lin[:, :, 1], edge_lin[:, :, 0], float(NB), hi_f, ALU.mult, ALU.add))
            go(v_.tensor_copy(dense_lin[:, :, 2], w_lin))
            go(v_.tensor_copy(prevf[:], prev_i))
            mark("edges_ready")
            go(v_.tensor_tensor(notst[:], dstf, prevf[:], ALU.is_equal))
            go(v_.tensor_scalar(negst[:], notst[:], 1.0, BIG, ALU.subtract, ALU.mult))
            go(v_.tensor_reduce(cnt[:, 0:1], notst[:], AX_X, ALU.min))
            go(v_.tensor_scalar(chain_in[:], ones[:, 0:2 * H], cnt[:, 0:1], None, ALU.mult))
            go(v_.memset(cnt[:, 0:1], 0.0))
            go(v_.memset(cnt[:, NB:NB + 1], float(E) / P))
            for b in range(1, NB):
                go(v_.tensor_scalar(bk[:, 0:C], dstf, float(b * NP), None, ALU.is_lt, ALU.add, accum_out=cnt[:, b:b + 1]))
            mark("cnt_ready")
            v.wait_ge(S["chain_tr"], 1)
            go(v_.tensor_copy(cf_sum[:], bank(4, 2 * H, P)))
            go(v_.tensor_copy(R[:], bank(3, P, NB + 1)))
            go(v_.tensor_scalar(cf_max[:], cf_sum[:], 1.0, BIG, ALU.subtract, ALU.mult))
            first, last, nst, off, delta, dd, tot = (small[:, j, 0:NB] for j in range(7))
            go(v_.tensor_scalar(last, R[:, 1:NB + 1], 1.0, None, ALU.subtract))
            go(v_.tensor_tensor(last, last, R[:, 0:NB], ALU.max))
            go(v_.tensor_copy(small_i[:, 0, 0:NB], R[:, 0:NB]))
            go(v_.tensor_copy(small_i[:, 1, 0:NB], last))
            go(v_.tensor_scalar(small_i[:, :, 0:NB], small_i[:, :, 0:NB], 7, None, ALU.logical_shift_right))
            go(v_.tensor_copy(first, small_i[:, 0, 0:NB]))
            go(v_.tensor_copy(last, small_i[:, 1, 0:NB]))
            go(v_.tensor_tensor(nst, last, first, ALU.subtract))
            go(v_.tensor_scalar(nst, nst, 1.0, None, ALU.add))
            go(v_.tensor_tensor_scan(tot, ones[:, 0:NB], nst, 0.0, ALU.mult, ALU.add))
            go(v_.tensor_tensor(off, tot, nst, ALU.subtract))
            go(v_.tensor_tensor(delta, first, off, ALU.subtract))
            go(v_.tensor_tensor(dd[:, 1:NB], delta[:, 1:NB], delta[:, 0:NB - 1], ALU.subtract))
            go(v_.tensor_copy(tk[:], tk2[:]))
            for b in range(1, NB):
                go(v_.tensor_scalar(small[:, 7, 0:KG], tk2[:], off[:, b:b + 1], dd[:, b:b + 1], ALU.is_ge, ALU.mult))
                go(v_.tensor_tensor(tk[:], tk[:], small[:, 7, 0:KG], ALU.add))
            go(v_.tensor_scalar(small[:, 7, 0:KG], tk2[:], tot[:, NB - 1:NB], float(PAD_TILE), ALU.is_ge, ALU.mult))
            go(v_.tensor_tensor(tk[:], tk[:], small[:, 7, 0:KG], ALU.add))
            go(v_.tensor_scalar(tk_i[:], tk[:], float(PAD_TILE), None, ALU.min))
            mark("tk_ready")
            go(v_.memset(bk[:], 0.0))
            for b in range(1, NB):
                go(v_.scalar_tensor_tensor(bk[:], iota_row[:], off[:, b:b + 1], bk[:], ALU.is_ge, ALU.add))
            go(v_.tensor_copy(bk_i[:], bk[0:1, :]))
            v.wait_ge(S["wtr"], 1)
            v.wait_ge(S["weights_in"], 16 * 12)
            v.wait_ge(S["vecs_in"], 16 * 8)
            go(v_.tensor_copy(w1T[:], bank(0, D, 3 * D)))
            go(v_.tensor_copy(embT[:], bank(1, D, RELS)))
            go(v_.tensor_copy(wmT[:], bank(5, D, D)))
            go(v_.tensor_scalar(bm_b[:], ones[0:D, :], bm_col[:, 0:1], None, ALU.mult))
            mark("wtr_sb")
            v.wait_ge(S["vproj"], 1)
            go(v_.tensor_copy(vv[:], bank(2, D, 3)))
            go(v_.tensor_copy(wmu[:], bank(2, D, D, P)))
            go(v_.tensor_copy(vec[:, BM, :], bank(2, P, D, 2 * P)))
            go(v_.tensor_copy(rhs0[:, D:D + 2], vv[:, 0:2]))
            go(v_.tensor_scalar(vr_b[:], ones[0:D, :], vv[:, 2:3], None, ALU.mult))
            v.wait_ge(S["x_in"], 16)
            v.wait_ge(S["vecs_in"], 16 * 8)
            v.wait_ge(S["weights_in"], 16 * 12)
            layer_norm(X[:], Hn[:])
            go(v_.tensor_scalar(Hn[:], Hn[:], 0.0, None, ALU.max))
            mark("h_ready")
            v.wait_ge(S["node_mm"], 1)
            for j in range(-(-NB // PERB)):
                n = min(PERB, NB - PERB * j)
                ps = bank(j, NP, PERB * P).rearrange("p (n c) -> p n c", c=P)
                go(v_.tensor_copy(T2[:, PERB * j:PERB * j + n, :], ps[:, 0:n, 0:D]))
                go(v_.tensor_copy(nfl[:, 0, PERB * j:PERB * j + n], ps[:, 0:n, D]))
                go(v_.tensor_copy(nfl[:, 1, PERB * j:PERB * j + n], ps[:, 0:n, D + 1]))
            v.wait_ge(S["edges_out"], 16)
            for b in range(NB):
                go(v_.tensor_scalar(big[0:NP, b * RELS:(b + 1) * RELS], bank(7, NP, RELS), nfl[:, 0, b:b + 1], None, ALU.add), False)
            mark("pair_ready")
            v.wait_ge(S["rows_sb"], ROW_UNITS[0])
            v.wait_ge(S["pair_out"], 16)
            t_f, s_f, w_f = (steps3[:, j * KP:(j + 1) * KP] for j in range(3))
            v1 = junk[:, 0:KP]
            go(v_.scalar_tensor_tensor(dstl[:], bk[:], -float(NP), t_f, ALU.mult, ALU.add))
            go(v_.tensor_copy(idx_src_k[:, 0:KP], s_f))
            go(v_.memset(w4[:, :, 0], 1.0))
            go(v_.tensor_copy(w4[:, :, 1], w_f))
            go(v_.tensor_tensor(v1, w_f, w4[:, :, 1], ALU.subtract))
            go(v_.tensor_copy(w4[:, :, 2], v1))
            go(v_.tensor_tensor(v1, v1, w4[:, :, 2], ALU.subtract))
            go(v_.tensor_copy(w4[:, :, 3], v1))
            go(v_.tensor_scalar(dst_b, dstl[:], -1.0, float(NP), ALU.max, ALU.min))
            go(v_.tensor_copy(iota_h.rearrange("p (c s) -> p c s", s=HALF), free(iota_row[:, 0:1], [[1, W], [0, HALF]])))
            mark("steps_ready")
            at_step = free(dst_b[:, 0:1], [[0, W], [1, KP]])
            with v.Fori(0, AGG_ITERS) as i:
                for h in range(2):
                    v.wait_ge(S["hist_used"], RING * i + HALF * (h + 1))
                    v_.tensor_tensor(free(s_bf[:, 0:1], [[HALF, W], [1, HALF]], h * W * HALF),
                                     iota_h.rearrange("p (c s) -> p c s", s=HALF), at_step[:, :, bass.ds(RING * i + HALF * h, HALF)],
                                     ALU.is_equal).then_inc(S["hist_s"], HALF)
            v.wait_ge(S["hist_used"], K + RING)
            hist = bank(7, NP, 4 * NB).rearrange("p (b k) -> p b k", k=4)
            go(v_.tensor_copy(deg[:], hist[:, :, 0]))
            go(v_.tensor_reduce(norm[:], hist[:, :, 1:4], AX_X, ALU.add))
            mark("tri_in")
            v.wait_ge(S["tri_done"], 1)
            start, has, tmp = nfl[:, 2, :], nfl[:, 3, :], st[:, 0, :]
            go(v_.tensor_tensor(start, bank(6, NP, NB), R[0:NP, 0:NB], ALU.add))
            go(v_.tensor_scalar(has, deg[:], 0.0, None, ALU.is_equal))
            go(v_.scalar_tensor_tensor(tmp, has, OUT_OF_RANGE, start, ALU.mult, ALU.add))
            go(v_.tensor_copy(start_i[:], tmp))
            go(v_.tensor_tensor(tmp, tmp, deg[:], ALU.add))
            go(v_.tensor_scalar(last_i[:], tmp, 1.0, None, ALU.subtract))
            mark("idx_ready")
            go(v_.tensor_tensor(rank_in.rearrange("p (b u) -> p b u", b=NB), bc(start, WB),
                                free(sel5[:, 0:1], [[0, NB], [1, WB]]), ALU.mult))
            mark("rank_in")
            v.wait_ge(S["r5_tr"], 1)
            R5, firsti, lasti, t0, n5, one, off5 = tw(0), tw(1, True), tw(2, True), tw(3), tw(4), tw(5), tw(6)
            go(v_.tensor_copy(R5[:, 0:NW // 2], bank(0, P, NW // 2)))
            go(v_.tensor_copy(R5[:, NW // 2:NW], bank(1, P, NW - NW // 2)))
            go(v_.memset(R5[:, NW:NW + 1], float(E)))
            go(v_.memset(one, 1.0))
            go(v_.tensor_scalar(t0[:, 0:NW], R5[:, 1:NW + 1], 1.0, None, ALU.subtract))
            go(v_.tensor_tensor(t0[:, 0:NW], t0[:, 0:NW], R5[:, 0:NW], ALU.max))
            go(v_.tensor_copy(firsti[:, 0:NW], R5[:, 0:NW]))
            go(v_.tensor_copy(lasti[:, 0:NW], t0[:, 0:NW]))
            for t_ in (firsti, lasti):
                go(v_.tensor_scalar(t_[:, 0:NW], t_[:, 0:NW], 7, None, ALU.logical_shift_right))
            go(v_.tensor_copy(R5[:, 0:NW], firsti[:, 0:NW]))
            go(v_.tensor_copy(t0[:, 0:NW], lasti[:, 0:NW]))
            go(v_.tensor_tensor(n5[:, 0:NW], t0[:, 0:NW], R5[:, 0:NW], ALU.subtract))
            go(v_.tensor_scalar(n5[:, 0:NW], n5[:, 0:NW], 1.0, None, ALU.add))
            n3 = n5[:, 0:NW].rearrange("p (b u) -> p b u", b=NB)
            for part in range(2):
                s_, r_, i_ = small[:, 0, 0:NB], small[:, 1, 0:NB], small_i[:, 0, 0:NB]
                go(v_.tensor_reduce(s_, n3[:, :, CUTS[part]:CUTS[part + 1]], AX_X, ALU.add))
                go(v_.tensor_scalar(i_, s_, float(UD - 1), None, ALU.add))
                go(v_.tensor_scalar(i_, i_, UD.bit_length() - 1, UD.bit_length() - 1, ALU.logical_shift_right, ALU.logical_shift_left))
                go(v_.tensor_copy(r_, i_))
                go(v_.tensor_tensor(r_, r_, s_, ALU.subtract))
                end = n3[:, :, CUTS[part + 1] - 1]
                go(v_.tensor_tensor(end, end, r_, ALU.add))
            go(v_.tensor_tensor_scan(t0[:, 0:NW], one[:, 0:NW], n5[:, 0:NW], 0.0, ALU.mult, ALU.add))
            go(v_.tensor_tensor(off5[:, 0:NW], t0[:, 0:NW], n5[:, 0:NW], ALU.subtract))
            go(v_.tensor_tensor(n5[:, 0:NW], R5[:, 0:NW], off5[:, 0:NW], ALU.subtract))
            dd5 = one
            go(v_.tensor_tensor(dd5[:, 1:NW], n5[:, 1:NW], n5[:, 0:NW - 1], ALU.subtract))
            cuts = cut_i[:, 0:2 * NB].rearrange("p (b k) -> p b k", k=2)
            for part in range(2):
                go(v_.tensor_copy(cuts[:, :, part], off5[0:1, 0:NW].rearrange("p (b u) -> p b u", b=NB)[:, :, CUTS[part]]))
            go(v_.tensor_copy(cut_i[:, 2 * NB:2 * NB + 1], t0[0:1, NW - 1:NW]))
            kf, kw, kt, kq, ku, kp = (k5[:, j, :] for j in range(6))
            go(v_.tensor_copy(kf, kg5_i[:]))
            for g in range(DG):
                go(v_.tensor_scalar(n5[:, 1:NW], off5[:, 1:NW], kf[:, g:g + 1], None, ALU.is_le, ALU.add, accum_out=kw[:, g:g + 1]))
                go(v_.scalar_tensor_tensor(n5[:, 1:NW], off5[:, 1:NW], kf[:, g:g + 1], dd5[:, 1:NW], ALU.is_le, ALU.mult))
                go(v_.tensor_reduce(kt[:, g:g + 1], n5[:, 1:NW], AX_X, ALU.add))
            go(v_.tensor_tensor(kt, kt, kf, ALU.add))
            go(v_.tensor_scalar(tk5_i[:], kt, float(PAD_TILE), None, ALU.min))
            mark("k5_ready")
            go(v_.tensor_scalar(kq, kw, 0.5, 1.0 / WB, ALU.add, ALU.mult))
            go(v_.tensor_scalar(tk2i[:], kq, 0.5, None, ALU.subtract))
            go(v_.tensor_copy(kq, tk2i[:]))
            go(v_.scalar_tensor_tensor(ku, kq, -float(WB), kw, ALU.mult, ALU.add))
            for op, at, add in ((ALU.is_ge, float(WB), -float(WB)), (ALU.is_lt, 0.0, float(WB)), (ALU.is_ge, float(CUTS[1]), -float(CUTS[1]))):
                go(v_.tensor_scalar(kq, ku, at, add, op, ALU.mult))
                go(v_.tensor_tensor(ku, ku, kq, ALU.add))
            go(v_.tensor_copy(kp, ku))
            v.wait_ge(S["drows_in"], 16 * DG)
            go(v_.tensor_scalar(kq, kw, float(WN * NB), None, ALU.mult))
            for g in range(DG):
                cc = free(drow[:, 0:1], [[3, P]], g * 3 * P + 1)
                go(v_.tensor_scalar(cc, cc, kq[:, g:g + 1], None, ALU.subtract))
            mark("k5_ready")
            v.wait_ge(S["kpos_tr"], 1)
            go(v_.tensor_copy(pos_c[:], bank(7, DG, P)))
            mark("kpos_sb")
            v.wait_ge(S["drows_sb"], D_UNITS)
            tab = tabs.rearrange("p (q k) -> p q k", q=5)
            go(v_.tensor_copy(tab[:, 0, :], d_lo))
            go(v_.tensor_scalar(tab[:, 1, :], d_c, -1.0, float(NP + 1), ALU.max, ALU.min))
            for q in range(2, 5):
                go(v_.tensor_copy(tab[:, q, :], d_w))
                if q < 4:
                    go(v_.tensor_tensor(d_w, d_w, tab[:, q, :], ALU.subtract))
            go(v_.tensor_copy(iota_q.rearrange("p (c s) -> p c s", s=QB), free(iota_row[:, 0:1], [[1, W], [0, QB]])))
            iota_2 = free(iota_q[:, 0:1], [[0, 2], [QB, W], [1, QB]])
            at_c, at_w = (free(tabs[:, 0:1], [[DP, n], [0, W], [1, DP]], q * DP) for q, n in ((0, 2), (2, 3)))
            mark("dense_ready")

            def dense_hots(k, halves=(0, 1)):
                for h in halves:
                    v.wait_ge(S["one_used"], k + QB * (h + 1))
                    v_.tensor_tensor(hot(h, 0, 2), iota_2, at_c[:, :, :, bass.ds(k + QB * h, QB)],
                                     ALU.is_equal).then_inc(S["hot_ready"], QB)
                    v.wait_ge(S["hot_ready"], k + QB * (h + 1))
                    target = free(hots[:, 0:1], [[0, 3], [QB, W], [1, QB]], (h * 5 + 1) * W * QB)
                    v_.tensor_tensor(hot(h, 2, 3), target, at_w[:, :, :, bass.ds(k + QB * h, QB)],
                                     ALU.mult).then_inc(S["one_ready"], QB)

            def share_out(part, end):
                v.wait_ge(S["one_used"], end + UD)
                v_.tensor_copy(share_sb(blk_c, part, 1), share_psum(0, part, 1))
                v_.tensor_copy(share_sb(blk_w, part, 1), share_psum(1, part, 1)).then_inc(S["share1_sb"], 1)

            def dense_block(b, first):
                for part in range(2):
                    at = [v.value_load(cut_i[0:1, bass.ds(2 * b + (part + j), 1)], min_val=0, max_val=KD) for j in range(2)]
                    dense_hots(at[0], (0,))
                    if part:
                        if not first:
                            v.wait_ge(S["blk_out"], 32 * b)
                        share_out(0, at[0])
                    elif not first:
                        share_out(1, at[0])
                    dense_hots(at[0], (1,))
                    with v.Fori(at[0] + UD, at[1], UD) as k:
                        dense_hots(k)

            dense_block(0, True)
            with v.Fori(1, NB) as b:
                dense_block(b, False)
            share_out(1, v.value_load(cut_i[0:1, 2 * NB:2 * NB + 1], min_val=0, max_val=KD))
            v.wait_ge(S["blk_out"], 32 * NB)

            chains = [0]

            def scan_all(buf, out_buf, w, flags, cf, op0, neutral):
                same = buf is out_buf
                for j in range(w):
                    if same:
                        go(v_.tensor_tensor_scan(junk[:, 0:C], flags[:], col(buf, j, w), neutral, op0[0], op0[1]))
                        go(v_.tensor_copy(ends[:, j:j + 1], junk[:, C - 1:C]))
                    else:
                        go(v_.tensor_tensor_scan(col(out_buf, j, w), flags[:], col(buf, j, w), neutral, op0[0], op0[1]), False)
                if not same:
                    v.wait_ge(S["dve"], done[0])
                    go(v_.tensor_copy(ends[:, 0:w], free(out_buf[:, 0:1], [[1, w]], (C - 1) * w)))
                n = chains[0]
                mark("ends_ready")
                v.wait_ge(S["ends_tr"], n + 1)
                go(v_.memset(carry_row[0:w, 0:1], neutral))
                go(v_.tensor_tensor_scan(carry_row[0:w, 1:P + 1], cf[0:w, :], bank(5, w, P), neutral, op0[0], op0[1]))
                mark("carry_in")
                v.wait_ge(S["carry_tr"], n + 1)
                go(v_.tensor_copy(carry[:, 0:w], bank(6, P, w)))
                for j in range(w):
                    go(v_.tensor_tensor_scan(col(out_buf, j, w), flags[:], col(buf, j, w), carry[:, j:j + 1], op0[0], op0[1]), False)
                chains[0] += 1

            MAXOP, SUMOP = (ALU.add, ALU.max), (ALU.mult, ALU.add)

            def softmax(turn, nh, slope):
                w = nh * C
                q = qa[:, 0:w]
                q3 = q.rearrange("p (c k) -> p c k", k=nh)
                fa = big[:, 0:2 * w].rearrange("p (c k) -> p c k", k=2 * nh)
                fb, sm = big[:, w:2 * w], big[:, 0:w]
                mx, den, fill, me = packed(nmx, nh), packed(nden, nh), packed(nfill, 2 * nh), packed(nself, nh)
                go(v_.memset(nmx[:], -BIG))
                go(v_.memset(nden[:], 0.0))
                mark("nmx_ready")
                if turn == 0:
                    for h in range(2):
                        v.wait_ge(S[f"q_out{h}"], 16 * LIN_ITERS)
                scan_all(q, sm, nh, negst, cf_max, MAXOP, -BIG)
                mark("scan_ready")
                v.wait_ge(S["nodes_in"], 16 * NB * (2 * turn + 1))
                if turn == 0:
                    go(v_.tensor_copy(fill[:, :, 0], nfl[:, 1, :]))
                else:
                    a_s, a_d = asd[:, :, 0:H], asd[:, :, H:2 * H]
                    go(v_.tensor_copy(fill[:, :, 0:nh], a_d))
                    go(v_.tensor_tensor(mx, mx, a_s, ALU.max))
                    go(v_.tensor_tensor(me, a_s, a_d, ALU.add))
                    go(v_.scalar_tensor_tensor(me, me, slope, me, ALU.mult, ALU.max))
                go(v_.tensor_tensor(mx, mx, fill[:, :, 0:nh], ALU.add))
                go(v_.scalar_tensor_tensor(fill[:, :, nh:2 * nh], mx, slope, mx, ALU.mult, ALU.max))
                if turn == 1:
                    go(v_.tensor_tensor(me, me, fill[:, :, nh:2 * nh], ALU.subtract))
                mark("fill_ready")
                v.wait_ge(S["fill_in"], 16 * (2 * turn + 1))
                fbuf = big[:, 0:2 * w]
                scan_all(fbuf, fbuf, 2 * nh, notst, cf_sum, SUMOP, 0.0)
                v.wait_ge(S["dve"], done[0])
                go(v_.tensor_tensor(q3, q3, fa[:, :, 0:nh], ALU.add))
                go(v_.scalar_tensor_tensor(q, q, slope, q, ALU.mult, ALU.max))
                go(v_.tensor_tensor(q3, q3, fa[:, :, nh:2 * nh], ALU.subtract))
                go(v_.tensor_scalar(q, q, 0.0, None, ALU.min))
                mark("exp_in")
                v.wait_ge(S["exp_done"], turn + 1)
                scan_all(q, sm, nh, notst, cf_sum, SUMOP, 0.0)
                mark("scan_ready")
                v.wait_ge(S["nodes_in"], 16 * NB * (2 * turn + 2))
                pack_b = packed(nfill, nh)
                if turn == 0:
                    go(v_.tensor_tensor(den, den, bc(nfl[:, 3, :], 1), ALU.add))
                    go(v_.reciprocal(pack_b, den))
                else:
                    go(v_.tensor_tensor(den, den, me, ALU.add))
                    go(v_.tensor_scalar(den, den, SM_EPS, float(nh), ALU.add, ALU.mult))
                    go(v_.reciprocal(pack_b, den))
                    go(v_.tensor_tensor(me, me, pack_b, ALU.mult))
                mark("fill_ready")
                v.wait_ge(S["fill_in"], 16 * (2 * turn + 2))
                scan_all(fb, fb, nh, notst, cf_sum, SUMOP, 0.0)
                v.wait_ge(S["dve"], done[0])
                go(v_.tensor_tensor(q, q, fb, ALU.mult))
                mark("alpha_ready")

            def one_hots(name, val):
                used = USED_BASE[name]
                with v.Fori(0, AGG_ITERS) as i:
                    for s in range(RING):
                        v.wait_ge(S["ring_used"], RING * i + (used + s + 1))
                        v_.tensor_scalar(s_ring[:, s, 0:NP], iota_row[:, 0:NP], dstl[:, bass.ds(RING * i + s, 1)],
                                         val[:, bass.ds(RING * i + s, 1)], ALU.is_equal, ALU.mult).then_inc(S["s_ready"], 1)
                v.wait_ge(S["ring_used"], used + K + RING)

            softmax(0, 1, 0.01)
            v.wait_ge(S["rows_sb"], ROW_BASE[1] + ROW_UNITS[1])
            one_hots("l0", alpha0)
            go(v_.tensor_tensor(T1[:], Hn[:], bc(nfl[:, 3, :], D), ALU.mult))
            go(v_.tensor_tensor(T1[:], T1[:], T2[:], ALU.add))
            go(v_.tensor_tensor(T1[:], T1[:], agg_psum(), ALU.add))
            go(v_.scalar_tensor_tensor(X[:], T1[:], 0.0, X[:], ALU.max, ALU.add))
            layer_norm(X[:], Hn[:])
            go(v_.tensor_scalar(Hn[:], Hn[:], 0.0, None, ALU.max))
            mark("h_ready")
            v.wait_ge(S["node_mm"], 2)
            go(v_.tensor_tensor(T1[:], agg_psum(), vb(BM), ALU.add))
            mark("tab_ready")
            v.wait_ge(S["ct_used"], 7 * (NB + 1))
            go(v_.tensor_tensor(T1[:], agg_psum(), vb(BU), ALU.add))
            go(v_.scalar_tensor_tensor(X[:], T1[:], 0.0, X[:], ALU.max, ALU.add))
            layer_norm(X[:], Hn[:])
            go(v_.tensor_scalar(Hn[:], Hn[:], 0.0, None, ALU.max))
            go(v_.tensor_scalar(st[:, 1, :], norm[:], 1.0, None, ALU.max))
            inv_root()
            go(v_.tensor_copy(norm[:], st[:, 3, :]))
            go(v_.tensor_tensor(T1[:], Hn[:], bc(norm[:], D), ALU.mult))
            mark("tab_ready")
            v.wait_ge(S["neigh_tr"], 1)
            go(v_.tensor_tensor(T1[:], agg_psum(), bc(norm[:], D), ALU.mult))
            go(v_.tensor_tensor(T2[:], Hn[:], T1[:], ALU.add))
            go(v_.tensor_tensor(T1[:], T1[:], bc(norm[:], D), ALU.mult))
            mark("tab_ready")
            v.wait_ge(S["neigh_tr"], 2)
            go(v_.tensor_tensor(T1[:], agg_psum(), bc(norm[:], D), ALU.mult))
            go(v_.tensor_tensor(T2[:], T2[:], T1[:], ALU.add))
            go(v_.scalar_tensor_tensor(X[:], T2[:], 1.0 / 3.0, X[:], ALU.mult, ALU.add))
            v.wait_ge(S["watt_in"], 32)
            for j in range(2):
                go(v_.tensor_tensor(big[0:D, 0:HD], watt[:], att_b[:, j, :], ALU.mult))
                go(v_.tensor_reduce(w_asd[:, j * H:(j + 1) * H], big[0:D, 0:HD].rearrange("p (h c) -> p h c", h=H), AX_X, ALU.add))
            mark("wasd_ready")
            layer_norm(X[:], Hn[:])
            go(v_.tensor_scalar(Hn[:], Hn[:], 0.0, None, ALU.max))
            mark("h_ready")
            v.wait_ge(S["node_mm"], 3)
            go(v_.tensor_copy(asd[:], bank(7, NP, 2 * H * NB).rearrange("p (b k) -> p b k", b=NB)))
            mark("asd_sb")
            v.wait_ge(S["y_out"], 16)
            go(v_.tensor_tensor(hot_hi.rearrange("p (c k) -> p c k", k=NB), free(iota_bf[:, 0:1], [[0, C], [1, NB]]),
                                free(hi_b[:, 0:1], [[1, C], [0, NB]]), ALU.is_equal))
            go(v_.tensor_copy(iota_look.rearrange("p (c s) -> p c s", s=CB), free(iota_row[:, 0:1], [[1, W], [0, CB]])))
            go(v_.tensor_copy(ident_bf, ident[:]))
            go(v_.tensor_copy(src_left.rearrange("p (h g) -> p h g", h=H), free(asd[:, 0, 0:1], [[1, H], [2 * H, NB]])))
            for r in range(3):
                part = src_parts[:, r * HN:(r + 1) * HN]
                go(v_.tensor_copy(part, src_left))
                if r < 2:
                    go(v_.tensor_tensor(src_left, src_left, part, ALU.subtract))
            at_look = free(lo_b[:, 0:1], [[0, W], [1, C]])
            hi_look = free(hot_hi[:, 0:1], [[NB, C], [0, H], [1, NB]])

            def look_hots(j, g):
                v.wait_ge(S["look_tr"], g + 1)
                v_.tensor_tensor(free(look_hot[:, 0:1], [[CB, W], [1, CB]], j * CB * W), iota_look.rearrange("p (c s) -> p c s", s=CB),
                                 at_look[:, :, bass.ds(CB * g, CB)], ALU.is_equal).then_inc(S["look_hot"], 1)

            def pick(j, g):
                v.wait_ge(S["look_mm"], g + (1 + 2))
                v.wait_ge(S["look_sum"], g + 1)
                v_.tensor_tensor(picked.rearrange("p (s h k) -> p s h k", s=CB, h=H),
                                 free(PS[:, 0:1], [[BANK // 2, CB], [NB, H], [1, NB]], 2 * j * BANK),
                                 hi_look[:, bass.ds(CB * g, CB), :, :], ALU.mult).then_inc(S["look_used"], 1)

            def sum_up(g):
                v.wait_ge(S["look_used"], g + (1 + 2))
                v_.tensor_reduce(qa[:, bass.ds(CB * H * g, CB * H)], picked.rearrange("p (s k) -> p s k", k=NB),
                                 AX_X, ALU.add).then_inc(S["look_sum"], 1)

            for j in range(2):
                look_hots(j, j)
            with v.Fori(0, LOOK_GROUPS // 2 - 1) as i:
                for j in range(2):
                    look_hots(j, 2 * i + (j + 2))
                    pick(j, 2 * i + j)
                    sum_up(2 * i + j)
            for j in range(2):
                pick(j, LOOK_GROUPS - 2 + j)
                sum_up(LOOK_GROUPS - 2 + j)
            v.wait_ge(S["look_sum"], LOOK_GROUPS + 1)
            softmax(1, H, 0.2)
            v.wait_ge(S["rows_sb"], ROW_BASE[2] + ROW_UNITS[2])
            base, used = BASE["l3"], USED_BASE["l3"]
            a3 = free(qa[:, 0:1], [[1, KP], [KP, H], [0, D]])
            target3 = free(dstl[:, 0:1], [[1, KP], [0, NP]])
            with v.Fori(0, AGG_ITERS) as i:
                for q in range(0, RING, MB):
                    pr = prod[:, q % PR:q % PR + MB, :]
                    for s in range(q, q + MB):
                        v.wait_ge(slot[s], 16 * i + 16 * (base + 1))
                    v.wait_ge(S["ring_used"], RING * i + (used + q + MB + RING - PR))
                    v_.tensor_tensor(pr.rearrange("p s (h f) -> p s h f", h=H),
                                     yring[:, q:q + MB, :].rearrange("p s (h f) -> p s h f", h=H),
                                     a3[:, bass.ds(RING * i + q, MB), :, :], ALU.mult).then_inc(S["prod_done"], MB)
                    v_.tensor_tensor(s_ring[:, q:q + MB, 0:NP], free(iota_row[:, 0:1], [[0, MB], [1, NP]]),
                                     target3[:, bass.ds(RING * i + q, MB), :], ALU.is_equal)
                    v.wait_ge(S["prod_done"], RING * i + q + MB)
                    v_.tensor_tensor(pr[:, :, 0:HD // 2], pr[:, :, 0:HD // 2], pr[:, :, HD // 2:HD],
                                     ALU.add).then_inc(S["s_ready"], MB)
            v.wait_ge(S["ring_used"], used + K + RING)
            v.wait_ge(S["y_back"], 16)
            y4 = big[0:NP, :].rearrange("p (k f) -> p k f", f=D)
            go(v_.tensor_tensor(y4, y4, free(nself[:, 0, 0:1], [[1, NB * H], [0, D]]), ALU.mult))
            go(v_.tensor_reduce(T2[:], big[0:NP, :].rearrange("p (b h f) -> p b f h", b=NB, h=H), AX_X, ALU.add))
            for j in range(2):
                go(v_.tensor_tensor(T2[:], T2[:], free(PS[0:NP, 0:1], [[2 * D, NB], [1, D]], j * D), ALU.add))
            go(v_.tensor_tensor(T2[:], T2[:], vb(BA), ALU.add))
            go(v_.tensor_tensor(T2[:], T2[:], Hn[:], ALU.add))
            layer_norm(T2[:], Hn[:])
            go(v_.tensor_tensor(Hn[:], Hn[:], vb(G1), ALU.mult))
            go(v_.tensor_tensor(Hn[:], Hn[:], vb(E1), ALU.add))
            mark("h_ready")
            v.wait_ge(S["node_mm"], 4)
            go(v_.tensor_tensor(T2[:], agg_psum(), vb(B2), ALU.add))
            go(v_.tensor_tensor(T2[:], T2[:], Hn[:], ALU.add))
            layer_norm(T2[:], Hn[:])
            go(v_.tensor_tensor(Hn[:], Hn[:], vb(G2), ALU.mult))
            go(v_.tensor_tensor(Hn[:], Hn[:], vb(E2), ALU.add))
            go(v_.tensor_tensor(X[:], X[:], Hn[:], ALU.add))
            mark("x_done")


_INS = ['x', 'src', 'dst', 'edge_type_200', 'edge_weight', 'L0_gnn_emb_rel', 'L0_gnn_loop_weight', 'L0_gnn_attn_w1',
        'L0_gnn_attn_w2', 'L1_gnn_W_msg', 'L1_gnn_b_msg', 'L1_gnn_W_upd', 'L1_gnn_b_upd', 'L3_gnn_W_att',
        'L3_gnn_att_src', 'L3_gnn_att_dst', 'L3_gnn_bias_att', 'L3_gnn_W1', 'L3_gnn_b1', 'L3_gnn_W2', 'L3_gnn_b2',
        'L3_gnn_ln1_g', 'L3_gnn_ln1_b', 'L3_gnn_ln2_g', 'L3_gnn_ln2_b']


def kernel(**inputs):
    import numpy as _np
    import concourse.bacc as _bacc
    from concourse import mybir as _mybir
    from concourse.bass_utils import run_bass_kernel_spmd as _run

    nc = _bacc.Bacc("TRN2", target_bir_lowering=False, num_devices=1)
    arrays, args = {}, []
    for name in _INS:
        a = _np.ascontiguousarray(inputs[name])
        arrays[f"in_{name}_dram"] = a
        args.append(nc.dram_tensor(f"in_{name}_dram", a.shape, _mybir.dt.from_np(a.dtype), kind="ExternalInput").ap())
    args.append(nc.dram_tensor("out_0_dram", inputs["x"].shape, _mybir.dt.float32, kind="ExternalOutput").ap())
    gnn_four_layers(nc, *args)
    r = _run(nc, [arrays], core_ids=[0])
    return r.results[0]["out_0_dram"]
```
